# Optimizing a Trainium2 kernel written in Bass

```python
import numpy as np
import jax
import jax.numpy as jnp

def _softmax(x, axis=-1):
    return jax.nn.softmax(x, axis=axis)

def _gelu(x):
    return jax.nn.gelu(x, approximate=True)

def _silu(x):
    return jax.nn.silu(x)

def _sigmoid(x):
    return jax.nn.sigmoid(x)

def _layernorm(x, axis=-1, eps=1e-05):
    m = jnp.mean(x, axis=axis, keepdims=True)
    v = jnp.var(x, axis=axis, keepdims=True)
    return (x - m) / jnp.sqrt(v + eps)

def _scatter_add(tgt, idx, src, axis=0):
    return tgt.at[idx].add(src)

def _segment_sum(src, seg, n):
    return jax.ops.segment_sum(src, seg, n)
kernel_name = 'mk_prb_d1_jaxref_r8_002e7b'

def setup_inputs(seed: int=0):
    np.random.seed(seed)
    _w = jnp.asarray

    def _L0_attn_setup():
        import jax, jax.numpy as jnp
        import numpy as np
        D_MODEL = 512
        N_Q = 32
        N_KV = 8
        HD = 128
        SLIDE = 64

        def _gqa_swa_attention(q, k, v, slide):
            B, Hq, N, D = q.shape
            Hkv = k.shape[1]
            G = Hq // Hkv
            qg = q.reshape(B, Hkv, G, N, D)
            scale = 1.0 / jnp.sqrt(jnp.asarray(D, q.dtype))
            s = jnp.einsum('bhgnd,bhmd->bhgnm', qg, k) * scale
            i = jnp.arange(N)[:, None]
            j = jnp.arange(N)[None, :]
            mask = j <= i
            if slide > 0:
                mask = mask & (i - j < slide)
            s = jnp.where(mask[None, None, None], s, jnp.asarray(-jnp.inf, s.dtype))
            p = jax.nn.softmax(s, axis=-1)
            o = jnp.einsum('bhgnm,bhmd->bhgnd', p, v)
            return o.reshape(B, Hq, N, D)
        key = jax.random.key(seed)
        ks = jax.random.split(key, 5)
        std = 0.01
        x = jax.random.normal(ks[0], (2, 256, D_MODEL), dtype=jnp.float32)
        wq = jax.random.normal(ks[1], (N_Q * HD, D_MODEL), dtype=jnp.float32) * std
        wk = jax.random.normal(ks[2], (N_KV * HD, D_MODEL), dtype=jnp.float32) * std
        wv = jax.random.normal(ks[3], (N_KV * HD, D_MODEL), dtype=jnp.float32) * std
        wo = jax.random.normal(ks[4], (D_MODEL, N_Q * HD), dtype=jnp.float32) * std
        return {'x': x, 'wq': wq, 'wk': wk, 'wv': wv, 'wo': wo}
    _L0_attn_in = _L0_attn_setup()

    def _L0_ffn_setup():
        import jax, jax.numpy as jnp
        import numpy as np
        TOP_K = 2
        key = jax.random.key(seed)
        k0, k1, k2 = jax.random.split(key, 3)
        B, S, D, H, E = (4, 256, 512, 512, 8)
        sc = 1.0 / np.sqrt(D).astype(np.float32)
        x = jax.random.normal(k0, (B, S, D), dtype=jnp.float32)
        W_gate = jax.random.normal(k1, (D, E), dtype=jnp.float32) * sc
        b_gate = jnp.zeros((E,), dtype=jnp.float32)
        W_e = jax.random.normal(k2, (E, D, H), dtype=jnp.float32) * sc
        b_e = jnp.zeros((E, H), dtype=jnp.float32)
        return {'x': x, 'W_gate': W_gate, 'b_gate': b_gate, 'W_e': W_e, 'b_e': b_e}
    _L0_ffn_in = _L0_ffn_setup()
    _d = {'L0_attn_x': _L0_attn_in['x'], 'L0_attn_wq': _L0_attn_in['wq'], 'L0_attn_wk': _L0_attn_in['wk'], 'L0_attn_wv': _L0_attn_in['wv'], 'L0_attn_wo': _L0_attn_in['wo'], 'L0_ffn_W_gate': _L0_ffn_in['W_gate'], 'L0_ffn_b_gate': _L0_ffn_in['b_gate'], 'L0_ffn_W_e': _L0_ffn_in['W_e'], 'L0_ffn_b_e': _L0_ffn_in['b_e']}
    _x0 = _d['L0_attn_x']
    _d['L0_attn_x'] = jax.random.normal(jax.random.fold_in(jax.random.key(seed), 1), (2, 512, 512), dtype=_x0.dtype)
    del _x0
    return _d

def reference(L0_attn_x, L0_attn_wq, L0_attn_wk, L0_attn_wv, L0_attn_wo, L0_ffn_W_gate, L0_ffn_b_gate, L0_ffn_W_e, L0_ffn_b_e):

    def _L0_attn_ref(x, wq, wk, wv, wo):
        import jax, jax.numpy as jnp
        import numpy as np
        D_MODEL = 512
        N_Q = 32
        N_KV = 8
        HD = 128
        SLIDE = 64

        def _gqa_swa_attention(q, k, v, slide):
            B, Hq, N, D = q.shape
            Hkv = k.shape[1]
            G = Hq // Hkv
            qg = q.reshape(B, Hkv, G, N, D)
            scale = 1.0 / jnp.sqrt(jnp.asarray(D, q.dtype))
            s = jnp.einsum('bhgnd,bhmd->bhgnm', qg, k) * scale
            i = jnp.arange(N)[:, None]
            j = jnp.arange(N)[None, :]
            mask = j <= i
            if slide > 0:
                mask = mask & (i - j < slide)
            s = jnp.where(mask[None, None, None], s, jnp.asarray(-jnp.inf, s.dtype))
            p = jax.nn.softmax(s, axis=-1)
            o = jnp.einsum('bhgnm,bhmd->bhgnd', p, v)
            return o.reshape(B, Hq, N, D)
        B, N, _ = x.shape
        q = (x @ wq.T).reshape(B, N, N_Q, HD).transpose(0, 2, 1, 3)
        k = (x @ wk.T).reshape(B, N, N_KV, HD).transpose(0, 2, 1, 3)
        v = (x @ wv.T).reshape(B, N, N_KV, HD).transpose(0, 2, 1, 3)
        o = _gqa_swa_attention(q, k, v, SLIDE)
        o = o.transpose(0, 2, 1, 3).reshape(B, N, N_Q * HD)
        return o @ wo.T

    def _L0_ffn_ref(x, W_gate, b_gate, W_e, b_e):
        import jax, jax.numpy as jnp
        import numpy as np
        TOP_K = 2
        logits = x @ W_gate + b_gate
        _, top_idx = jax.lax.top_k(logits, TOP_K)
        y_all = jax.nn.relu(jnp.einsum('bsd,edh->bseh', x, W_e) + b_e)
        y = jnp.take_along_axis(y_all, top_idx[..., None], axis=2)
        return y.mean(axis=2)
    x = L0_attn_x
    xn = _layernorm(x, axis=-1)
    x = x + _L0_attn_ref(xn, L0_attn_wq, L0_attn_wk, L0_attn_wv, L0_attn_wo) + _L0_ffn_ref(xn, L0_ffn_W_gate, L0_ffn_b_gate, L0_ffn_W_e, L0_ffn_b_e)
    return x

_drawn_inputs = setup_inputs


def setup_inputs(seed=0):
    import zlib

    import numpy as np

    out = dict(_drawn_inputs(seed))
    spreads = {'L0_ffn_b_gate': (0.0, 0.1), 'L0_ffn_b_e': (0.0, 0.1)}
    factors = {'L0_attn_wq': 8.0, 'L0_attn_wk': 8.0, 'L0_attn_wv': 3.003, 'L0_attn_wo': 2.969}
    for name, (base, spread) in spreads.items():
        noise = np.random.default_rng([zlib.crc32(name.encode()), seed]).standard_normal(out[name].shape)
        drawn = base * np.exp(spread * noise) if base else spread * noise
        out[name] = jnp.asarray(drawn.astype(out[name].dtype))
    for name, factor in factors.items():
        out[name] = (out[name] * factor).astype(out[name].dtype)
    return out
```

```python
import concourse.bass as bass
from concourse import mybir
from contextlib import ExitStack

P = 128
NB, NTOK, DM = 2, 512, 512
T = NB * NTOK // P
TB = NTOK // P
KC = DM // P
HD = 128
HG = 4
G = 8
W = 64
NJ = NTOK // W
KCOLS = W + NTOK
NEG = -3.0e38
EPS = 1e-5
ITEMS = 16
CHUNKS = 7
FREE = 1
SLOT = [0, 1, 2, 0, 1, 2, 1]


def build(nc, x, wq, wk, wv, wo, wg, bg, we, be, out):
    fp32 = mybir.dt.float32
    f32r = mybir.dt.float32r
    u32 = mybir.dt.uint32
    ALU = mybir.AluOpType
    ACT = mybir.ActivationFunctionType
    AX = mybir.AxisListType
    SCALE = float(HD) ** -0.5

    ctx = ExitStack()
    with ctx:
        def sb(name, shape, dt=fp32):
            return ctx.enter_context(nc.sbuf_tensor(name, shape, dt))

        def pair(name, shape):
            return sb(name + "_hi", shape, f32r), sb(name + "_lo", shape, f32r)

        def sem(name):
            return ctx.enter_context(nc.semaphore(name))

        xT = pair("xT", [P, KC, T * P])
        w_kv = pair("w_kv", [P, 2, KC, P])
        w_q = pair("w_q", [P, HG, KC, P])
        w_e = pair("w_e", [P, KC, DM])
        w_o = pair("w_o", [P, HG, DM])
        stage = sb("stage", [P, 3, 1024])
        kT = pair("kT", [P, NB, KCOLS])
        vT = sb("vT", [P, NB, KCOLS])
        v = pair("v", [P, NB * NJ, HD])
        qT = pair("qT", [P, NJ, HG, W])
        sm = sb("sm", [P, 2, 4, P])
        pr = sb("pr", [P, 2, 4, P])
        pT = pair("pT", [P, 2, HG, W])
        oT = pair("oT", [P, HG, P])
        acc = sb("acc", [P, T, DM])
        y = sb("y", [P, DM])
        be_b = sb("be_b", [P, DM])
        ident = sb("ident", [P, P])
        mask = sb("mask", [P, 2, P])
        wg_f = sb("wg_f", [P, KC, G])
        wg_s = pair("wg_s", [P, KC, G])
        bg_b = sb("bg_b", [P, G])
        iota_e = sb("iota_e", [P, G])
        stats = sb("stats", [P, T, 6])
        mv = sb("mv", [P, T, 2])
        ve = sb("ve", [P, T])
        sd = sb("sd", [P, T])
        rs = sb("rs", [P, T])
        tmp = sb("tmp", [P, T])
        lg = sb("lg", [P, T, G])
        top = sb("top", [P, T, 8])
        topi = sb("topi", [P, T, 8], u32)
        topf = sb("topf", [P, T, 2])
        eq = sb("eq", [P, T, 2, G])
        gate = sb("gate", [P, G, T])
        gate_g = sb("gate_g", [P, T])
        nmax = sb("nmax", [P, 2, 4])
        rsum = sb("rsum", [P, 2, 4])
        rinv = sb("rinv", [P, 4])
        carry = sb("carry", [P, 1])

        def bank(name):
            return ctx.enter_context(nc.psum_tensor(name, [P, 512], fp32))
        p_item = [bank("p_item0"), bank("p_item1")]
        p_s = [bank("p_s0"), bank("p_s1")]
        p_pt, p_o, p_out, p_y = bank("p_pt"), bank("p_o"), bank("p_out"), bank("p_y")

        x_in = [sem(f"x_in{i}") for i in range(T)]
        small_in = sem("small_in")
        w_in = [sem(f"w_in{i}") for i in range(3)]
        be_in = sem("be_in")
        w_split = sem("w_split")
        consts = sem("consts")
        wg_hi_done, wg_done = sem("wg_hi_done"), sem("wg_done")
        pool_chain = sem("pool_chain")
        split_hi = sem("split_hi")
        ln_var, ln_sd, ln_xn = sem("ln_var"), sem("ln_sd"), sem("ln_xn")
        ln_t, ln_hi, ln_lo, ln_lg = sem("ln_t"), sem("ln_hi"), sem("ln_lo"), sem("ln_lg")
        lg_read = sem("lg_read")
        dve_chain = sem("dve_chain")
        item_mm = sem("item_mm")
        item_hi = sem("item_hi")
        item_out = sem("item_out")
        s_mm, s_read, s_max = sem("s_mm"), sem("s_read"), sem("s_max")
        p_exp, p_inv, p_norm = sem("p_exp"), sem("p_inv"), sem("p_norm")
        pt_mm, pt_hi, pt_lo = sem("pt_mm"), sem("pt_hi"), sem("pt_lo")
        o_mm, o_hi, o_lo = sem("o_mm"), sem("o_hi"), sem("o_lo")
        out_mm, out_acc = sem("out_mm"), sem("out_acc")
        y_mm, y_bias, y_relu, y_acc = sem("y_mm"), sem("y_bias"), sem("y_relu"), sem("y_acc")
        gate_done = sem("gate_done")
        stored = sem("stored")

        ITEM = [("k", 0), ("k", 1), ("v", 0), ("v", 1)]
        for i in range(HG):
            ITEM += [("q", i), ("t", i)]
        ITEM += [("q", HG + i) for i in range(HG)]
        HI_COUNT = [sum(k != "v" for k, _ in ITEM[:i + 1]) for i in range(ITEMS)]
        Q1 = ITEMS - HG
        F = lambda a: a.bitcast(fp32)

        block = ctx.enter_context(nc.Block())

        @block.sync
        def _(sp):
            for t in range(T):
                sp.dma_start(acc[:, t, :], x[t * P:(t + 1) * P, :]).then_inc(x_in[t], 16)
            sp.dma_start(wg_f[:, :, :], wg.rearrange("(k p) e -> p k e", p=P)).then_inc(small_in, 16)
            sp.dma_start(bg_b[:, :], bg.partition_broadcast(P)).then_inc(small_in, 16)
            with sp.Fori(0, G) as g:
                src = [(stage[:, 0, 0:512], wk[g, :, :]), (stage[:, 0, 512:1024], wv[g, :, :]),
                       (stage[:, 1, :], wq[g, :, 0:1024]), (stage[:, 2, :], wq[g, :, 1024:2048])]
                sp.wait_ge(w_split, FREE + g * CHUNKS)
                for dst, s in src[:2]:
                    sp.dma_start(dst, s).then_inc(w_in[0], 16)
                for slot, (dst, s) in enumerate(src[2:]):
                    sp.dma_start(dst, s).then_inc(w_in[1 + slot], 16)
                sp.wait_ge(y_bias, FREE + g * T)
                sp.dma_start(be_b[:, :], be[g, :].partition_broadcast(P)).then_inc(be_in, 16)
                late = [we[g, :, 0:1024], we[g, :, 1024:2048], wo[g, :, 0:1024], wo[g, :, 1024:2048]]
                for c, s in zip(range(3, CHUNKS), late):
                    prev = max(i for i in range(c) if SLOT[i] == SLOT[c])
                    sp.wait_ge(w_split, FREE + g * CHUNKS + prev + 1)
                    sp.dma_start(stage[:, SLOT[c], :], s).then_inc(w_in[SLOT[c]], 16)
            for t in range(T):
                sp.wait_ge(out_acc, FREE + (G - 1) * T + t + 1)
                sp.dma_start(out[t * P:(t + 1) * P, :], acc[:, t, :]).then_inc(stored, 16)
            sp.wait_ge(stored, 16 * T)

        @block.gpsimd
        def _(pool):
            pool.sem_inc(w_split, FREE)
            chain = [0]

            def link(ins):
                chain[0] += 1
                ins.then_inc(pool_chain, 1)
                pool.wait_ge(pool_chain, chain[0])

            link(nc.gpsimd.memset(ident[:, :], 0.0))
            link(nc.gpsimd.affine_select(out=ident[:, :], in_=ident[:, :], compare_op=ALU.not_equal, fill=1.0,
                                         base=0, pattern=[[-1, P]], channel_multiplier=1))
            link(nc.gpsimd.memset(mask[:, :, :], 0.0))
            for half in range(2):
                m = mask[half * W:(half + 1) * W, :, :]
                link(nc.gpsimd.affine_select(out=m, in_=m, compare_op=ALU.is_gt, fill=NEG, base=0,
                                             pattern=[[0, 2], [1, P]], channel_multiplier=-1))
                link(nc.gpsimd.affine_select(out=m, in_=m, compare_op=ALU.is_ge, fill=NEG, base=W,
                                             pattern=[[0, 2], [-1, P]], channel_multiplier=1))
            link(nc.gpsimd.memset(mask[:, 0, 0:W], NEG))
            for b in range(NB):
                nc.gpsimd.memset(F(kT[0])[:, b, 0:W], 0.0)
                nc.gpsimd.memset(F(kT[1])[:, b, 0:W], 0.0)
                nc.gpsimd.memset(vT[:, b, 0:W], 0.0)
            nc.gpsimd.iota(iota_e[:, :], pattern=[[1, G]], base=0, channel_multiplier=0,
                           allow_small_or_imprecise_dtypes=True).then_inc(consts, 1)
            pool.wait_ge(consts, 1)
            pool.wait_ge(small_in, 32)
            nc.gpsimd.tensor_copy(wg_s[0][:, :, :], wg_f[:, :, :]).then_inc(wg_hi_done, 1)
            pool.wait_ge(wg_hi_done, 1)
            nc.gpsimd.tensor_tensor(wg_s[1][:, :, :], wg_f[:, :, :], F(wg_s[0])[:, :, :],
                                    ALU.subtract).then_inc(wg_done, 1)
            dst = [[h[:, :, :, :].rearrange("p a k m -> p (a k m)") for h in w_kv],
                   [h[:, 0:2, :, :].rearrange("p a k m -> p (a k m)") for h in w_q],
                   [h[:, 2:4, :, :].rearrange("p a k m -> p (a k m)") for h in w_q],
                   [h[:, 0:2, :].rearrange("p k m -> p (k m)") for h in w_e],
                   [h[:, 2:4, :].rearrange("p k m -> p (k m)") for h in w_e],
                   [h[:, 0:2, :].rearrange("p k m -> p (k m)") for h in w_o],
                   [h[:, 2:4, :].rearrange("p k m -> p (k m)") for h in w_o]]
            PER_SLOT = [3, 3, 2]
            with pool.Fori(0, G) as g:
                seen = [0, 0, 0]
                for c in range(CHUNKS):
                    s = SLOT[c]
                    seen[s] += 2 if c == 0 else 1
                    pool.wait_ge(w_in[s], g * (16 * PER_SLOT[s]) + 16 * seen[s])
                    if c == 0:
                        pool.wait_ge(item_mm, FREE + g * ITEMS)
                    if c == 3:
                        pool.wait_ge(y_mm, FREE + g * T)
                    if c == 5:
                        pool.wait_ge(out_mm, FREE + g * T)
                    hi, lo = dst[c]
                    nc.gpsimd.tensor_tensor(carry[:, :], iota_e[:, 0:1], iota_e[:, 0:1], ALU.add)
                    nc.gpsimd.tensor_copy(hi, stage[:, s, :]).then_inc(split_hi, 1)
                    pool.wait_ge(split_hi, g * CHUNKS + c + 1)
                    nc.gpsimd.tensor_tensor(lo, stage[:, s, :], hi.bitcast(fp32),
                                            ALU.subtract).then_inc(w_split, 1)

        @block.scalar
        def _(act):
            for signal in (item_hi, p_exp, pt_hi, o_hi, y_relu):
                act.sem_inc(signal, FREE)
            act.wait_ge(ln_var, 1)
            nc.scalar.activation(sd[:, :], ve[:, :], ACT.Sqrt).then_inc(ln_sd, 1)
            for t in range(T):
                act.wait_ge(ln_t, t + 1)
                nc.scalar.copy(xT[0][:, :, t * P:(t + 1) * P],
                               [p_pt, p_o][t % 2][:, :].rearrange("p (k c) -> p k c", k=KC)).then_inc(ln_hi, 1)

            def item(g, i):
                kind, n = ITEM[i]
                if kind == "v":
                    return
                act.wait_ge(item_mm, FREE + g * ITEMS + i + 1)
                src = p_item[i % 2]
                if kind == "k":
                    nc.scalar.copy(kT[0][:, n, W:KCOLS], src[:, :]).then_inc(item_hi, 1)
                elif kind == "q":
                    nc.scalar.copy(qT[0][:, :, n % HG, :],
                                   src[:, :].rearrange("p (j q) -> p j q", j=NJ)).then_inc(item_hi, 1)
                else:
                    nc.scalar.copy(v[0][:, 4 * n:4 * n + 4, :],
                                   src[:, :].rearrange("p (j d) -> p j d", j=4)).then_inc(item_hi, 1)

            with act.Fori(0, G) as g:
                for i in range(Q1):
                    item(g, i)
                for s in range(T + 1):
                    if s < T:
                        act.wait_ge(s_max, FREE + g * T + s + 1)
                        if s >= 2:
                            act.wait_ge(pt_mm, FREE + g * T + s - 1)
                        for c in range(4):
                            e = nc.scalar.activation(pr[:, s % 2, c, :], sm[:, s % 2, c, :], ACT.Exp,
                                                     bias=nmax[:, s % 2, c:c + 1], scale=1.0,
                                                     accum_out=rsum[:, s % 2, c:c + 1])
                        e.then_inc(p_exp, 1)
                    if s == TB - 1:
                        for i in range(Q1, ITEMS):
                            item(g, i)
                    if s >= 1:
                        act.wait_ge(pt_mm, FREE + g * T + s)
                        nc.scalar.copy(pT[0][:, :, :, :].rearrange("p j h q -> p (j h q)"),
                                       p_pt[:, :]).then_inc(pt_hi, 1)
                    if s < T:
                        act.wait_ge(y_bias, FREE + g * T + s + 1)
                        if s == 0:
                            act.wait_ge(gate_done, FREE + g + 1)
                            act.wait_ge(y_acc, FREE + g * T)
                        else:
                            act.wait_ge(y_acc, FREE + g * T + s)
                        nc.scalar.activation(y[:, :], p_y[:, :], ACT.Relu,
                                             scale=gate_g[:, s:s + 1]).then_inc(y_relu, 1)
                    if s >= 1:
                        act.wait_ge(o_mm, FREE + g * T + s)
                        nc.scalar.copy(oT[0][:, :, :].rearrange("p h (j q) -> p j h q", j=2),
                                       p_o[:, :].rearrange("p (j h q) -> p j h q", j=2, h=HG)).then_inc(o_hi, 1)

        @block.vector
        def _(dve):
            for signal in (item_out, s_read, s_max, p_inv, p_norm, pt_lo, o_lo, out_acc, y_bias, y_acc, gate_done):
                dve.sem_inc(signal, FREE)
            chain = [0]

            def link(ins):
                chain[0] += 1
                ins.then_inc(dve_chain, 1)
                dve.wait_ge(dve_chain, chain[0])

            for t in range(T):
                dve.wait_ge(x_in[t], 16)
                nc.vector.bn_stats(stats[:, t, :], acc[:, t, :]).then_inc(dve_chain, 1)
                chain[0] += 1
            dve.wait_ge(dve_chain, chain[0])
            for t in range(T):
                last = nc.vector.bn_aggr(mv[:, t, :], stats[:, t, :])
            link(last)
            nc.vector.tensor_scalar(ve[:, :], mv[:, :, 1], EPS, None, ALU.add).then_inc(ln_var, 1)
            dve.wait_ge(ln_sd, 1)
            link(nc.vector.reciprocal(rs[:, :], sd[:, :]))
            link(nc.vector.tensor_tensor(tmp[:, :], rs[:, :], rs[:, :], ALU.mult))
            link(nc.vector.tensor_tensor(tmp[:, :], tmp[:, :], ve[:, :], ALU.mult))
            link(nc.vector.tensor_scalar(tmp[:, :], tmp[:, :], -0.5, 1.5, ALU.mult, ALU.add))
            link(nc.vector.tensor_tensor(rs[:, :], rs[:, :], tmp[:, :], ALU.mult))

            def xlo(t):
                dve.wait_ge(ln_hi, t + 1)
                hi = xT[0][:, :, t * P:(t + 1) * P]
                nc.vector.tensor_tensor(xT[1][:, :, t * P:(t + 1) * P],
                                        [p_pt, p_o][t % 2][:, :].rearrange("p (k c) -> p k c", k=KC),
                                        F(hi), ALU.subtract).then_inc(ln_lo, 1)

            for t in range(T):
                if t >= 2:
                    dve.wait_ge(ln_t, t - 1)
                nc.vector.tensor_scalar(pr[:, t % 2, :, :].rearrange("p c n -> p (c n)"), acc[:, t, :],
                                        mv[:, t, 0:1], rs[:, t:t + 1],
                                        ALU.subtract, ALU.mult).then_inc(ln_xn, 1)
                if t >= 1:
                    xlo(t - 1)
            xlo(T - 1)
            dve.wait_ge(ln_lg, T)
            dve.wait_ge(small_in, 32)
            nc.vector.tensor_tensor(lg[:, :, :], p_y[:, 0:T * G].rearrange("p (t e) -> p t e", t=T),
                                    bg_b[:, :].unsqueeze(1).to_broadcast([P, T, G]), ALU.add).then_inc(lg_read, 1)
            dve.wait_ge(lg_read, 1)
            for t in range(T):
                last = nc.vector.max(top[:, t, :], lg[:, t, :])
            link(last)
            for t in range(T):
                last = nc.vector.max_index(topi[:, t, :], top[:, t, :], lg[:, t, :])
            link(last)
            link(nc.vector.tensor_copy(topf[:, :, :], topi[:, :, 0:2]))
            dve.wait_ge(consts, 1)
            for t in range(T):
                for k in range(2):
                    last = nc.vector.tensor_scalar(eq[:, t, k, :], iota_e[:, :], topf[:, t, k:k + 1], 0.5,
                                                   ALU.is_equal, ALU.mult)
            link(last)
            link(nc.vector.tensor_tensor(gate[:, :, :].rearrange("p e t -> p t e"), eq[:, :, 0, :],
                                         eq[:, :, 1, :], ALU.add))

            def item(g, i):
                kind, n = ITEM[i]
                src = p_item[i % 2]
                if kind == "v":
                    dve.wait_ge(item_mm, FREE + g * ITEMS + i + 1)
                    nc.vector.tensor_copy(vT[:, n, W:KCOLS], src[:, :]).then_inc(item_out, 1)
                    return
                dve.wait_ge(item_hi, FREE + g * HI_COUNT[-1] + HI_COUNT[i])
                if kind == "k":
                    nc.vector.tensor_tensor(kT[1][:, n, W:KCOLS], src[:, :], F(kT[0])[:, n, W:KCOLS],
                                            ALU.subtract).then_inc(item_out, 1)
                elif kind == "q":
                    nc.vector.tensor_tensor(qT[1][:, :, n % HG, :], src[:, :].rearrange("p (j q) -> p j q", j=NJ),
                                            F(qT[0])[:, :, n % HG, :], ALU.subtract).then_inc(item_out, 1)
                else:
                    nc.vector.tensor_tensor(v[1][:, 4 * n:4 * n + 4, :],
                                            src[:, :].rearrange("p (j d) -> p j d", j=4),
                                            F(v[0])[:, 4 * n:4 * n + 4, :], ALU.subtract).then_inc(item_out, 1)

            with dve.Fori(0, G) as g:
                dve.wait_ge(y_relu, FREE + g * T)
                nc.vector.tensor_copy(gate_g[:, :], gate[:, bass.ds(g, 1), :].rearrange("p o t -> p (o t)")
                                      ).then_inc(gate_done, 1)
                for i in range(Q1):
                    item(g, i)
                for s in range(T + 2):
                    if s < T:
                        dve.wait_ge(s_mm, FREE + g * T + s + 1)
                        if s >= 2:
                            dve.wait_ge(p_exp, FREE + g * T + s - 1)
                        ps = p_s[s % 2][:, :].rearrange("p (j c) -> p j c", j=2)
                        for jj in range(2):
                            kind = 0 if s % TB == 0 and jj == 0 else 1
                            m = mask[:, kind:kind + 1, :].to_broadcast([P, 2, P])
                            last = nc.vector.scalar_tensor_tensor(
                                sm[:, s % 2, 2 * jj:2 * jj + 2, :],
                                p_s[s % 2][:, jj * 256:jj * 256 + 256].rearrange("p (c n) -> p c n", c=2),
                                SCALE, m, ALU.mult, ALU.add)
                        last.then_inc(s_read, 1)
                        dve.wait_ge(s_read, FREE + g * T + s + 1)
                        nc.vector.tensor_reduce(nmax[:, s % 2, :], sm[:, s % 2, :, :], AX.X, ALU.max,
                                                negate=True).then_inc(s_max, 1)
                    if s == TB - 1:
                        for i in range(Q1, ITEMS):
                            item(g, i)
                    if s < T:
                        dve.wait_ge(y_mm, FREE + g * T + s + 1)
                        if s == 0:
                            dve.wait_ge(be_in, g * 16 + 16)
                        nc.vector.tensor_tensor(p_y[:, :], p_y[:, :], be_b[:, :], ALU.add).then_inc(y_bias, 1)
                        dve.wait_ge(p_exp, FREE + g * T + s + 1)
                        nc.vector.reciprocal(rinv[:, :], rsum[:, s % 2, :]).then_inc(p_inv, 1)
                        dve.wait_ge(p_inv, FREE + g * T + s + 1)
                        nc.vector.tensor_tensor(pr[:, s % 2, :, :], pr[:, s % 2, :, :],
                                                rinv[:, :].unsqueeze(2).to_broadcast([P, 4, P]),
                                                ALU.mult).then_inc(p_norm, 1)
                    if 1 <= s <= T:
                        dve.wait_ge(pt_hi, FREE + g * T + s)
                        nc.vector.tensor_tensor(pT[1][:, :, :, :].rearrange("p j h q -> p (j h q)"), p_pt[:, :],
                                                F(pT[0])[:, :, :, :].rearrange("p j h q -> p (j h q)"),
                                                ALU.subtract).then_inc(pt_lo, 1)
                    if s >= 2:
                        u = s - 2
                        dve.wait_ge(out_mm, FREE + g * T + u + 1)
                        dve.wait_ge(y_acc, FREE + g * T + u + 1)
                        nc.vector.tensor_tensor(acc[:, u, :], p_out[:, :], acc[:, u, :], ALU.add).then_inc(out_acc, 1)
                    if s < T:
                        dve.wait_ge(y_relu, FREE + g * T + s + 1)
                        if s == 0:
                            dve.wait_ge(out_acc, FREE + g * T)
                        nc.vector.tensor_tensor(acc[:, s, :], y[:, :], acc[:, s, :], ALU.add).then_inc(y_acc, 1)
                    if 1 <= s <= T:
                        dve.wait_ge(o_hi, FREE + g * T + s)
                        nc.vector.tensor_tensor(oT[1][:, :, :].rearrange("p h (j q) -> p j h q", j=2),
                                                p_o[:, :].rearrange("p (j h q) -> p j h q", j=2, h=HG),
                                                F(oT[0])[:, :, :].rearrange("p h (j q) -> p j h q", j=2),
                                                ALU.subtract).then_inc(o_lo, 1)

        @block.tensor
        def _(pe):
            for signal in (item_mm, s_mm, pt_mm, o_mm, out_mm, y_mm):
                pe.sem_inc(signal, FREE)
            def product(out_ap, terms):
                n = 0
                for (ah, al), (bh, bl) in terms:
                    for a, b in ((ah, bh), (ah, bl), (al, bh)):
                        n += 1
                        last = nc.tensor.matmul(out_ap, a, b, start=(n == 1), stop=(n == 3 * len(terms)))
                return last

            def cut(halves, *index):
                return halves[0][index], halves[1][index]

            A = slice(None)

            pe.wait_ge(consts, 1)
            for t in range(T):
                pe.wait_ge(ln_xn, t + 1)
                if t >= 2:
                    pe.wait_ge(ln_lo, t - 1)
                for k in range(KC):
                    last = nc.tensor.transpose([p_pt, p_o][t % 2][:, k * P:(k + 1) * P], pr[:, t % 2, k, :], ident[:, :])
                last.then_inc(ln_t, 1)
            pe.wait_ge(wg_done, 1)
            for t in range(T):
                pe.wait_ge(ln_lo, t + 1)
                n = 0
                for k in range(KC):
                    for a in xT:
                        for b in wg_s:
                            n += 1
                            last = nc.tensor.matmul(p_y[:, t * G:(t + 1) * G], a[:, k, t * P:(t + 1) * P], b[:, k, :],
                                                    start=(n == 1), stop=(n == 4 * KC))
                last.then_inc(ln_lg, 1)

            def item(g, i):
                kind, n = ITEM[i]
                dst = p_item[i % 2]
                if i == 0:
                    pe.wait_ge(w_split, FREE + g * CHUNKS + 1)
                if i == 4:
                    pe.wait_ge(w_split, FREE + g * CHUNKS + 3)
                pe.wait_ge(item_out, FREE + g * ITEMS + max(i - 1, 0))
                if kind == "t":
                    b, half = divmod(n, 2)
                    if n % 2 == 0:
                        pe.wait_ge(item_out, FREE + g * ITEMS + 3 + b)
                    for c in range(4):
                        j = half * 4 + c
                        last = nc.tensor.transpose(dst[:, c * P:(c + 1) * P], vT[:, b, j * W:j * W + P], ident[:, :])
                else:
                    b = n // HG if kind == "q" else n
                    w, m = {"k": (w_kv, 0), "v": (w_kv, 1), "q": (w_q, n % HG)}[kind]
                    last = product(dst[:, :], [(cut(w, A, m, k, A), cut(xT, A, k, slice(b * NTOK, (b + 1) * NTOK)))
                                               for k in range(KC)])
                last.then_inc(item_mm, 1)

            with pe.Fori(0, G) as g:
                for i in range(Q1):
                    item(g, i)
                for s in range(T + 2):
                    if s < T:
                        b, t = divmod(s, TB)
                        pe.wait_ge(item_out, FREE + g * ITEMS + (Q1 if b == 0 else ITEMS))
                        pe.wait_ge(s_read, FREE + g * T + max(s - 1, 0))
                        for c in range(4):
                            j, hp = 2 * t + c // 2, c % 2
                            last = product(p_s[s % 2][:, c * P:(c + 1) * P],
                                           [(cut(qT, A, j, slice(2 * hp, 2 * hp + 2), A),
                                             cut(kT, A, b, slice(j * W, j * W + P)))])
                        last.then_inc(s_mm, 1)
                        if s == TB - 1:
                            for i in range(Q1, ITEMS):
                                item(g, i)
                        if s == 0:
                            pe.wait_ge(w_split, FREE + g * CHUNKS + 5)
                            pe.wait_ge(lg_read, 1)
                        pe.wait_ge(y_relu, FREE + g * T + s)
                        product(p_y[:, :], [(cut(xT, A, k, slice(s * P, (s + 1) * P)), cut(w_e, A, k, A))
                                            for k in range(KC)]).then_inc(y_mm, 1)
                    if 1 <= s <= T:
                        u = s - 1
                        pe.wait_ge(p_norm, FREE + g * T + u + 1)
                        pe.wait_ge(pt_lo, FREE + g * T + u)
                        for c in range(4):
                            last = nc.tensor.transpose(p_pt[:, c * P:(c + 1) * P], pr[:, u % 2, c, :], ident[:, :])
                        last.then_inc(pt_mm, 1)
                    if s >= 2:
                        u = s - 2
                        if u == 0:
                            pe.wait_ge(w_split, FREE + g * CHUNKS + 7)
                        pe.wait_ge(o_lo, FREE + g * T + u + 1)
                        pe.wait_ge(out_acc, FREE + g * T + u)
                        product(p_out[:, :], [(cut(oT, A, h, A), cut(w_o, A, h, A)) for h in range(HG)]
                                ).then_inc(out_mm, 1)
                    if 1 <= s <= T:
                        u = s - 1
                        b, t = divmod(u, TB)
                        pe.wait_ge(pt_lo, FREE + g * T + u + 1)
                        pe.wait_ge(o_lo, FREE + g * T + u)
                        for jj in range(2):
                            last = product(p_o[:, jj * 256:(jj + 1) * 256],
                                           [(cut(v, A, b * NJ + 2 * t + jj, A), cut(pT, A, jj, A, A))])
                        last.then_inc(o_mm, 1)


def kernel(**inputs):
    import numpy as np
    import concourse.bacc as bacc
    from concourse.bass_utils import run_bass_kernel_spmd as run

    def arr(name):
        return np.asarray(inputs[name])

    def heads(w, n):
        return np.ascontiguousarray(w.reshape(G, n, HD, KC, P).transpose(0, 4, 1, 3, 2).reshape(G, P, n * KC * HD))

    a = {
        "x": np.ascontiguousarray(arr("L0_attn_x").reshape(NB * NTOK, DM)),
        "wq": heads(arr("L0_attn_wq"), HG),
        "wk": heads(arr("L0_attn_wk"), 1),
        "wv": heads(arr("L0_attn_wv"), 1),
        "wo": np.ascontiguousarray(arr("L0_attn_wo").reshape(DM, G, HG, HD).transpose(1, 3, 2, 0)
                                   .reshape(G, HD, HG * DM)),
        "wg": np.ascontiguousarray(arr("L0_ffn_W_gate")),
        "bg": np.ascontiguousarray(arr("L0_ffn_b_gate")),
        "we": np.ascontiguousarray(arr("L0_ffn_W_e").reshape(G, KC, P, DM).transpose(0, 2, 1, 3)
                                   .reshape(G, P, KC * DM)),
        "be": np.ascontiguousarray(arr("L0_ffn_b_e")),
    }
    nc = bacc.Bacc("TRN2", target_bir_lowering=False, num_devices=1)
    args = [nc.dram_tensor(f"in_{n}", v.shape, mybir.dt.from_np(v.dtype), kind="ExternalInput").ap()
            for n, v in a.items()]
    args.append(nc.dram_tensor("out_0", (NB * NTOK, DM), mybir.dt.float32, kind="ExternalOutput").ap())
    build(nc, *args)
    r = run(nc, [{f"in_{n}": v for n, v in a.items()}], core_ids=[0])
    return r.results[0]["out_0"].reshape(NB, NTOK, DM)
```

```python
import concourse.bass as bass
from concourse import mybir
from contextlib import ExitStack

P = 128
NB, NTOK, DM = 2, 512, 512
ROWS = NB * NTOK
T = ROWS // P
TB = NTOK // P
KC = DM // P
HD = 128
HG = 4
G = 8
E = 8
W = 64
NJ = NTOK // W
KCOLS = W + NTOK
MT = 24
MP = MT // G
NEG = -3.0e38
EPS = 1e-5

ITEM = [("k", 0), ("v", 0), ("q", 0), ("t", 0), ("q", 1), ("t", 1), ("q", 2), ("q", 3)]
NI = len(ITEM)
HI_COUNT = [sum(k != "v" for k, _ in ITEM[:i + 1]) for i in range(NI)]
NH = HI_COUNT[-1]
STEPS = T + 2
ITEMS_1 = {0: [0, 1], 1: [2, 3], 2: [4, 5], 3: [6, 7]}
ITEMS_0 = {5: [0, 1], 6: [2, 3], 7: [4, 5], 8: [6], 9: [7]}
X_STEP = {1: 0, 3: 1, 5: 2}
Y_STEP = {2: 0, 4: 1, 7: 2}
XG_BUF = [0, 1, 0]
CHUNKS = ["e0a", "e0b", "o0", "o1", "e1a", "e1b", "kv", "q0", "q1", "e2a", "e2b"]
SLOT = {"e0a": 0, "e0b": 1, "o0": 2, "o1": 3, "e1a": 0, "e1b": 1, "kv": 2, "q0": 3, "q1": 0, "e2a": 1, "e2b": 2}
FIRST = ["kv", "q0", "q1"]
NC, NF = len(CHUNKS), len(FIRST)
FREE = 1


def chunks_of(last):
    return [c for c in CHUNKS if not (last and c in FIRST)]


def split_count(g, name, last=False):
    return NF + g * NC + chunks_of(last).index(name) + 1


def arrived(g, name, last=False):
    slot = SLOT[name]
    ahead = sum(SLOT[c] == slot for c in FIRST)
    a_pass = sum(SLOT[c] == slot for c in CHUNKS)
    order = chunks_of(last)
    return 16 * ahead + g * (16 * a_pass) + 16 * sum(SLOT[c] == slot for c in order[:order.index(name) + 1])


def build(nc, x, wq, wkv, wo, wg, bg, we, be, out):
    fp32, f32r, bf16 = mybir.dt.float32, mybir.dt.float32r, mybir.dt.bfloat16
    u32, i32 = mybir.dt.uint32, mybir.dt.int32
    ALU = mybir.AluOpType
    ACT = mybir.ActivationFunctionType
    AX = mybir.AxisListType
    SCALE = float(HD) ** -0.5

    xn_rows = nc.dram_tensor("xn_rows", (ROWS + P, DM), fp32, kind="Internal").ap()
    y_rows = nc.dram_tensor("y_rows", (ROWS + P, DM), fp32, kind="Internal").ap()
    table = nc.dram_tensor("slot_tokens", (P * MT, 1), i32, kind="Internal").ap()
    NZ = 3

    ctx = ExitStack()
    with ctx:
        def sb(name, shape, dt=fp32):
            return ctx.enter_context(nc.sbuf_tensor(name, shape, dt))

        def pair(name, shape):
            return sb(name + "_hi", shape, f32r), sb(name + "_lo", shape, f32r)

        def sem(name):
            return ctx.enter_context(nc.semaphore(name))

        xT = pair("xT", [P, KC, ROWS])
        w_kv = pair("w_kv", [P, 2, KC, P])
        w_q = pair("w_q", [P, HG, KC, P])
        w_o = pair("w_o", [P, HG, DM])
        w_e = pair("w_e", [P, KC, DM])
        stage = sb("stage", [P, 4, 1024])
        kT = pair("kT", [P, NB, KCOLS])
        vT = sb("vT", [P, KCOLS])
        v = pair("v", [P, NB * NJ, HD])
        qT = pair("qT", [P, NB, NJ, HG, W])
        ring = sb("ring", [P, 4, DM])
        pr = ring[:, 0:2, :].rearrange("p b (c n) -> p b c n", c=4)
        xg = ring[:, 2:4, :]
        pT = pair("pT", [P, 2, HG, W])
        oT = pair("oT", [P, HG, P])
        xgT = pair("xgT", [P, KC, P])
        acc = sb("acc", [P, T, DM])
        y = sb("y", [P, DM])
        be_b = sb("be_b", [P, DM])
        ident = sb("ident", [P, P])
        mask = sb("mask", [P, 2, P])
        nmax = sb("nmax", [P, 2, 4])
        rsum = sb("rsum", [P, 2, 4])
        rinv = sb("rinv", [P, 4])
        carry = sb("carry", [P, 3 * MP + 1])
        stats = be_b[:, 192:240].rearrange("p (t n) -> p t n", n=6)
        mv = sb("mv", [P, T, 2])
        ve, sd, rs, tmp = (sb(n, [P, T]) for n in ("ve", "sd", "rs", "tmp"))
        wg_f = be_b[:, 320:352].rearrange("p (k e) -> p k e", e=E)
        bg_b = sb("bg_b", [P, E])
        fold = sb("fold", [P, E])
        below = sb("below", [P, P], bf16)
        ones = sb("ones", [P, P], bf16)
        member = sb("member", [P, T, E], bf16)
        iota_e = sb("iota_e", [P, E])
        iota_t = sb("iota_t", [P, MT])
        steps = sb("steps", [P, 8])
        before = be_b[:, 256:320].rearrange("p (e f) -> p e f", f=E)
        lg = be_b[:, 0:64].rearrange("p (t e) -> p t e", e=E)
        top = be_b[:, 64:128].rearrange("p (t n) -> p t n", n=8)
        topi = be_b[:, 128:192].bitcast(u32).rearrange("p (t n) -> p t n", n=8)
        topf = sb("topf", [P, T, 2])
        tiles_e, tile0, tile1 = (sb(n, [P, E]) for n in ("tiles_e", "tile0", "tile1"))
        expert_f = sb("expert_f", [P, MT])
        expert = sb("expert", [P, MT], i32)
        rank, rtile, rfull, rpos = (sb(n, [P, 2 * T]) for n in ("rank", "rtile", "rfull", "rpos"))
        slot = sb("slot", [P, 2 * T], u32)
        token = sb("token", [P, T], i32)
        no_token = sb("no_token", [P, MT], i32)
        slot_token = sb("slot_token", [P, MT], u32)
        idx = [sb(f"idx{c}", [P, 1], u32) for c in range(MP)]
        scratch = ring[:, 0:2, :].rearrange("p b n -> p (b n)")
        is_top = scratch[:, 0:128].rearrange("p (a e) -> p a e", e=E)
        prod = scratch[:, 128:256].rearrange("p (a e) -> p a e", e=E)
        cmp_q = scratch[:, 256:368].rearrange("p (a j) -> p a j", j=7)
        cmp_n = scratch[:, 384:448].rearrange("p (e j) -> p e j", j=8)
        prod_e = scratch[:, 448:512].rearrange("p (e f) -> p e f", f=E)
        cmp_t = scratch[:, 512:704].rearrange("p (i e) -> p i e", e=E)
        prod2 = scratch[:, 704:832].rearrange("p (a e) -> p a e", e=E)
        lgT = stage[:, 1, :]
        y_in = stage[:, :, :].rearrange("p s (t n) -> p (s t) n", n=DM)

        def bank(name):
            return ctx.enter_context(nc.psum_tensor(name, [P, 512], fp32))
        p_item = [bank("p_item0"), bank("p_item1")]
        p_s = [bank("p_s0"), bank("p_s1")]
        p_pt, p_o, p_out, p_y = bank("p_pt"), bank("p_o"), bank("p_out"), bank("p_y")
        p_ln = [p_pt, p_o]

        x_in = [sem(f"x_in{i}") for i in range(T)]
        small_in = sem("small_in")
        w_in = [sem(f"w_in{i}") for i in range(4)]
        w_hi, w_split = sem("w_hi"), sem("w_split")
        be_in = sem("be_in")
        consts, wg_done, pool_chain, dve_chain = sem("consts"), sem("wg_done"), sem("pool_chain"), sem("dve_chain")
        cleared = sem("cleared")
        ln_var, ln_sd, ln_xn = sem("ln_var"), sem("ln_sd"), sem("ln_xn")
        ln_t, ln_hi, ln_lo = sem("ln_t"), sem("ln_hi"), sem("ln_lo")
        xn_kept = [sem(f"xn_kept{i}") for i in range(4)]
        pad_kept = sem("pad_kept")
        lgT_mm, lgT_out, lg_mm, lg_read = sem("lgT_mm"), sem("lgT_out"), sem("lg_mm"), sem("lg_read")
        member_done, rank_mm, routed = sem("member_done"), sem("rank_mm"), sem("routed")
        table_clear, table_done, table_in = sem("table_clear"), sem("table_done"), sem("table_in")
        item_mm, item_hi, item_out = sem("item_mm"), sem("item_hi"), sem("item_out")
        s_mm, s_read, s_max = sem("s_mm"), sem("s_read"), sem("s_max")
        p_exp, p_inv, p_norm = sem("p_exp"), sem("p_inv"), sem("p_norm")
        pt_mm, pt_hi, pt_lo = sem("pt_mm"), sem("pt_hi"), sem("pt_lo")
        o_mm, o_hi, o_lo = sem("o_mm"), sem("o_hi"), sem("o_lo")
        out_mm, out_acc = sem("out_mm"), sem("out_acc")
        idx_done = sem("idx_done")
        xg_in = [sem("xg_in0"), sem("xg_in1")]
        x_mm, x_hi, x_lo = sem("x_mm"), sem("x_hi"), sem("x_lo")
        y_mm, y_bias, y_relu = sem("y_mm"), sem("y_bias"), sem("y_relu")
        y_added = sem("y_added")
        summed, stored = sem("summed"), sem("stored")

        def F(a):
            return a.bitcast(fp32)

        def nth(g, half, i):
            return g * (2 * NI) + half * NI + i

        def items_in(step, last):
            return ([(1, i) for i in ITEMS_1.get(step, [])]
                    + [(2, i) for i in ITEMS_0.get(step, []) if not last])

        def unit(g, u):
            return FREE + g * T + u

        def tile(g, c):
            return FREE + g * MP + c

        block = ctx.enter_context(nc.Block())

        @block.sync
        def _(sp):
            for t in range(T):
                sp.dma_start(acc[:, t, :], x[t * P:(t + 1) * P, :]).then_inc(x_in[t], 16)
            sp.dma_start(wg_f[:, :, :], wg.rearrange("(k p) e -> p k e", p=P)).then_inc(small_in, 16)
            sp.dma_start(bg_b[:, :], bg.partition_broadcast(P)).then_inc(small_in, 16)
            att = {"kv": lambda g: wkv[g, :, :], "q0": lambda g: wq[g, :, 0:1024], "q1": lambda g: wq[g, :, 1024:2048],
                   "o0": lambda g: wo[g, :, 0:1024], "o1": lambda g: wo[g, :, 1024:2048]}
            for c in FIRST:
                sp.dma_start(stage[:, SLOT[c], :], att[c](0)).then_inc(w_in[SLOT[c]], 16)
            sp.wait_ge(cleared, 1)
            sp.dma_start(xn_rows[ROWS:ROWS + P, :], y[:, :]).then_inc(pad_kept, 16)
            sp.dma_start(table.rearrange("(p i) o -> p (i o)", p=P), no_token[:, :]).then_inc(table_clear, 16)
            for t in range(T):
                sp.wait_ge(ln_xn, t + 1)
                sp.dma_start(xn_rows[t * P:(t + 1) * P, :], ring[:, t % 4, :]).then_inc(xn_kept[t % 4], 16)
            sp.wait_ge(table_done, 16 * 2 * T)
            sp.dma_start(slot_token[:, :], table.rearrange("(p i) o -> p (i o)", p=P).bitcast(u32)).then_inc(table_in, 16)
            sp.wait_ge(lg_read, 1)
            sp.wait_ge(routed, 1)

            def a_pass(g, last):
                order = chunks_of(last)
                for n, name in enumerate(order):
                    s = SLOT[name]
                    prev = [c for c in order[:n] if SLOT[c] == s]
                    sp.wait_ge(w_split, split_count(g, prev[-1], last) if prev else NF + g * NC)
                    if name[0] == "e":
                        c, half = int(name[1]), "ab".index(name[2])
                        if half == 0:
                            e = sp.value_load(expert[0:1, bass.ds(g * MP + c, 1)], min_val=0, max_val=E - 1)
                        src = we[bass.ds(e, 1), :, half * 1024:(half + 1) * 1024].rearrange("o p n -> (o p) n")
                        sp.dma_start(stage[:, s, :], src).then_inc(w_in[s], 16)
                        if half == 1:
                            sp.wait_ge(y_bias, tile(g, c))
                            sp.dma_start(be_b[:, :], be[bass.ds(e, 1), :].rearrange("o n -> (o n)").partition_broadcast(P)
                                         ).then_inc(be_in, 16)
                    else:
                        sp.dma_start(stage[:, s, :], att[name](g + 1 if name in FIRST else g)).then_inc(w_in[s], 16)

            with sp.Fori(0, G - 1) as g:
                a_pass(g, False)
            a_pass(G - 1, True)
            sp.wait_ge(y_added, 16 * (NZ + MT))
            sp.wait_ge(w_split, split_count(G - 1, "e2b", True))
            for t in range(T):
                sp.dma_start(y_in[:, t, :], y_rows[t * P:(t + 1) * P, :]).then_inc(x_in[t], 16)
            for t in range(T):
                sp.wait_ge(summed, t + 1)
                sp.dma_start(out[t * P:(t + 1) * P, :], acc[:, t, :]).then_inc(stored, 16)
            sp.wait_ge(stored, 16 * T)

        @block.gpsimd
        def _(pool):
            pool.sem_inc(idx_done, FREE)
            chain = [0]

            def link(ins):
                chain[0] += 1
                ins.then_inc(pool_chain, 1)
                pool.wait_ge(pool_chain, chain[0])

            def select(a, op, fill, base, pattern, mult):
                link(nc.gpsimd.affine_select(out=a, in_=a, compare_op=op, fill=fill, base=base,
                                             pattern=pattern, channel_multiplier=mult))

            def iota(a, pattern, base, mult):
                nc.gpsimd.iota(a, pattern=pattern, base=base, channel_multiplier=mult,
                               allow_small_or_imprecise_dtypes=True)

            link(nc.gpsimd.memset(ident[:, :], 0.0))
            select(ident[:, :], ALU.not_equal, 1.0, 0, [[-1, P]], 1)
            nc.gpsimd.memset(y[:, :], 0.0)
            iota(no_token[:, :], [[0, MT]], ROWS, 1)
            link(nc.gpsimd.memset(fold[:, :], 0.0))
            select(fold[:, :], ALU.not_equal, 1.0, 0, [[-1, E]], 1)
            select(fold[:, :], ALU.not_equal, 1.0, -E, [[-1, E]], 1)
            nc.gpsimd.memset(F(xgT[0])[:, :, :], 0.0).then_inc(cleared, 1)
            pool.wait_ge(cleared, 1)
            pool.wait_ge(small_in, 32)
            link(nc.gpsimd.tensor_copy(xgT[0][:, :, 0:E], wg_f[:, :, :]))
            nc.gpsimd.tensor_tensor(xgT[0][:, :, E:2 * E], wg_f[:, :, :], F(xgT[0])[:, :, 0:E],
                                    ALU.subtract).then_inc(wg_done, 1)
            for b in range(NB):
                nc.gpsimd.memset(F(kT[0])[:, b, 0:W], 0.0)
                nc.gpsimd.memset(F(kT[1])[:, b, 0:W], 0.0)
            nc.gpsimd.memset(vT[:, 0:W], 0.0)
            iota(iota_e[:, :], [[1, E]], 0, 0)
            iota(iota_t[:, :], [[1, MT]], 0, 0)
            iota(steps[:, :], [[P, 8]], 0, 0)
            iota(token[:, :], [[P, T]], 0, 1)
            link(nc.gpsimd.memset(ones[:, :], 1.0))
            link(nc.gpsimd.memset(below[:, :], 1.0))
            select(below[:, :], ALU.is_gt, 0.0, 0, [[1, P]], -1)
            link(nc.gpsimd.memset(before[:, :, :], 1.0))
            select(before[:, :, :], ALU.is_gt, 0.0, 0, [[1, E], [-1, E]], 0)
            nc.gpsimd.tensor_tensor(carry[:, 0:1], iota_e[:, 0:1], iota_e[:, 0:1], ALU.add).then_inc(consts, 1)
            carried = [0]

            halves = {"kv": [h[:, :, :, :].rearrange("p a k m -> p (a k m)") for h in w_kv]}
            for n in range(2):
                halves[f"q{n}"] = [h[:, 2 * n:2 * n + 2, :, :].rearrange("p a k m -> p (a k m)") for h in w_q]
                halves[f"o{n}"] = [h[:, 2 * n:2 * n + 2, :].rearrange("p k m -> p (k m)") for h in w_o]
                for c in range(MP):
                    halves[f"e{c}{'ab'[n]}"] = [h[:, 2 * n:2 * n + 2, :].rearrange("p k m -> p (k m)") for h in w_e]

            def lo(name, count):
                pool.wait_ge(w_hi, count)
                hi_ap, lo_ap = halves[name]
                nc.gpsimd.tensor_tensor(lo_ap, stage[:, SLOT[name], :], F(hi_ap), ALU.subtract).then_inc(w_split, 1)

            def held():
                carried[0] = carried[0] % (3 * MP) + 1
                n = carried[0]
                nc.gpsimd.tensor_tensor(carry[:, n:n + 1], iota_e[:, 0:1], iota_e[:, 0:1], ALU.add)

            lo("kv", 1)
            lo("q0", 2)
            link(nc.gpsimd.memset(mask[:, :, :], 0.0))
            for half in range(2):
                m = mask[half * W:(half + 1) * W, :, :]
                select(m, ALU.is_gt, NEG, 0, [[0, 2], [1, P]], -1)
                select(m, ALU.is_ge, NEG, W, [[0, 2], [-1, P]], 1)
            link(nc.gpsimd.memset(mask[:, 0, 0:W], NEG))
            lo("q1", 3)
            y_parts = y_rows.rearrange("(z n p) d -> z p n d", z=NZ, p=P)
            for z in range(NZ):
                nc.gpsimd.dma_start(y_parts[z, :, :, :], y[:, :].unsqueeze(1).to_broadcast([P, (ROWS + P) // P // NZ, DM])
                                    ).then_inc(y_added, 16)
            pool.wait_ge(table_clear, 16)
            pool.wait_ge(routed, 1)
            for t in range(T):
                for k in range(2):
                    nc.gpsimd.indirect_dma_start(table, bass.IndirectOffsetOnAxis(ap=slot[:, 2 * t + k:2 * t + k + 1], axis=0),
                                                 token[:, t:t + 1], None).then_inc(table_done, 16)
            pool.wait_ge(table_in, 16)
            pool.wait_ge(pad_kept, 16)
            for s in range(4):
                pool.wait_ge(xn_kept[s], 16 * (T // 4))

            def gather(g, c):
                pool.wait_ge(y_added, 16 * (NZ - MP + 1) + g * (16 * MP) + 16 * c)
                pool.wait_ge(x_mm, tile(g, 0) if c < 2 else tile(g, 1))
                held()
                nc.gpsimd.tensor_copy(idx[c][:, :], slot_token[:, bass.ds(g * MP + c, 1)]).then_inc(idx_done, 1)
                pool.wait_ge(idx_done, tile(g, c) + 1)
                held()
                nc.gpsimd.indirect_dma_start(xg[:, XG_BUF[c], :], None, xn_rows,
                                             bass.IndirectOffsetOnAxis(ap=idx[c][:, 0:1], axis=0)
                                             ).then_inc(xg_in[XG_BUF[c]], 16)

            def add(g, c):
                pool.wait_ge(y_relu, tile(g, c) + 1)
                pool.wait_ge(y_added, 16 * NZ + g * (16 * MP) + 16 * c)
                held()
                nc.gpsimd.indirect_dma_start(y_rows, bass.IndirectOffsetOnAxis(ap=idx[c][:, 0:1], axis=0),
                                             y[:, :], None, compute_op=ALU.add).then_inc(y_added, 16)

            def a_pass(g, last):
                gather(g, 0)
                gather(g, 1)
                for name in ("e0a", "e0b", "o0", "o1"):
                    lo(name, split_count(g, name, last))
                add(g, 0)
                for name in ("e1a", "e1b"):
                    lo(name, split_count(g, name, last))
                gather(g, 2)
                if not last:
                    for name in FIRST:
                        lo(name, split_count(g, name))
                add(g, 1)
                for name in ("e2a", "e2b"):
                    lo(name, split_count(g, name, last))
                add(g, 2)

            with pool.Fori(0, G - 1) as g:
                a_pass(g, False)
            a_pass(G - 1, True)

        @block.scalar
        def _(act):
            for signal in (p_exp, pt_hi, o_hi, x_hi, y_relu):
                act.sem_inc(signal, FREE)
            hi_of = {"kv": w_kv[0][:, :, :, :].rearrange("p a k m -> p (a k m)")}
            for n in range(2):
                hi_of[f"q{n}"] = w_q[0][:, 2 * n:2 * n + 2, :, :].rearrange("p a k m -> p (a k m)")
                hi_of[f"o{n}"] = w_o[0][:, 2 * n:2 * n + 2, :].rearrange("p k m -> p (k m)")
                for c in range(MP):
                    hi_of[f"e{c}{'ab'[n]}"] = w_e[0][:, 2 * n:2 * n + 2, :].rearrange("p k m -> p (k m)")

            def hi(name, count):
                act.wait_ge(w_in[SLOT[name]], count)
                nc.scalar.copy(hi_of[name], stage[:, SLOT[name], :]).then_inc(w_hi, 1)

            def item(g, half, i):
                kind, n = ITEM[i]
                if kind == "v":
                    return
                b = half % 2
                act.wait_ge(item_mm, nth(g, half, i) + 1)
                src = p_item[i % 2]
                if kind == "k":
                    nc.scalar.copy(kT[0][:, b, W:KCOLS], src[:, :]).then_inc(item_hi, 1)
                elif kind == "q":
                    nc.scalar.copy(qT[0][:, b, :, n, :],
                                   src[:, :].rearrange("p (j q) -> p j q", j=NJ)).then_inc(item_hi, 1)
                else:
                    nc.scalar.copy(v[0][:, b * NJ + 4 * n:b * NJ + 4 * n + 4, :],
                                   src[:, :].rearrange("p (j d) -> p j d", j=4)).then_inc(item_hi, 1)

            act.wait_ge(ln_var, 1)
            nc.scalar.activation(sd[:, :], ve[:, :], ACT.Sqrt).then_inc(ln_sd, 1)
            hi("kv", 16)
            for t in range(T):
                act.wait_ge(ln_t, t + 1)
                nc.scalar.copy(xT[0][:, :, t * P:(t + 1) * P],
                               p_ln[t % 2][:, :].rearrange("p (k c) -> p k c", k=KC)).then_inc(ln_hi, 1)
                if t == 1:
                    hi("q0", 16)
                if t == 3:
                    hi("q1", 16)
            for h in range(2):
                act.wait_ge(lgT_mm, h + 1)
                nc.scalar.copy(lgT[:, h * 512:(h + 1) * 512], p_s[h][:, :]).then_inc(lgT_out, 1)
            for i in range(NI):
                item(0, 0, i)

            def a_pass(g, last):
                act.wait_ge(y_mm, tile(g, 0))
                for name in ("e0a", "e0b"):
                    hi(name, arrived(g, name, last))
                for s in range(STEPS):
                    if s < T:
                        act.wait_ge(s_max, unit(g, s + 1))
                        act.wait_ge(pt_mm, unit(g, max(s - 1, 0)))
                        for c in range(4):
                            e = nc.scalar.activation(pr[:, s % 2, c, :], p_s[s % 2][:, c * P:(c + 1) * P], ACT.Exp,
                                                     bias=nmax[:, s % 2, c:c + 1], scale=1.0,
                                                     accum_out=rsum[:, s % 2, c:c + 1])
                        e.then_inc(p_exp, 1)
                    for half, i in items_in(s, last):
                        item(g, half, i)
                    if s == 0:
                        act.wait_ge(out_mm, unit(g, 0))
                        for name in ("o0", "o1"):
                            hi(name, arrived(g, name, last))
                    if s in X_STEP:
                        act.wait_ge(x_mm, tile(g, X_STEP[s]) + 1)
                        nc.scalar.copy(xgT[0][:, :, :].rearrange("p k c -> p (k c)"), p_y[:, :]).then_inc(x_hi, 1)
                    if 1 <= s <= T:
                        act.wait_ge(pt_mm, unit(g, s))
                        nc.scalar.copy(pT[0][:, :, :, :].rearrange("p j h q -> p (j h q)"),
                                       p_pt[:, :]).then_inc(pt_hi, 1)
                    if s in Y_STEP:
                        c = Y_STEP[s]
                        act.wait_ge(y_bias, tile(g, c) + 1)
                        act.wait_ge(y_added, 16 * NZ + g * (16 * MP) + 16 * c)
                        nc.scalar.activation(y[:, :], p_y[:, :], ACT.Relu, scale=0.5).then_inc(y_relu, 1)
                    if 1 <= s <= T:
                        act.wait_ge(o_mm, unit(g, s))
                        nc.scalar.copy(oT[0][:, :, :].rearrange("p h (j q) -> p j h q", j=2),
                                       p_o[:, :].rearrange("p (j h q) -> p j h q", j=2, h=HG)).then_inc(o_hi, 1)
                    if s in (2, 4):
                        act.wait_ge(y_mm, tile(g, s // 2))
                        for name in (f"e{s // 2}a", f"e{s // 2}b"):
                            hi(name, arrived(g, name, last))
                    if s == 3 and not last:
                        act.wait_ge(item_mm, nth(g, 2, 0))
                        for name in FIRST:
                            hi(name, arrived(g, name))

            with act.Fori(0, G - 1) as g:
                a_pass(g, False)
            a_pass(G - 1, True)

        @block.vector
        def _(dve):
            for signal in (s_read, s_max, p_inv, p_norm, pt_lo, o_lo, out_acc, x_lo, y_bias):
                dve.sem_inc(signal, FREE)
            chain = [0]

            def link(ins):
                chain[0] += 1
                ins.then_inc(dve_chain, 1)
                dve.wait_ge(dve_chain, chain[0])

            def item(g, half, i):
                kind, n = ITEM[i]
                b = half % 2
                src = p_item[i % 2]
                if kind == "v":
                    dve.wait_ge(item_mm, nth(g, half, i) + 1)
                    nc.vector.tensor_copy(vT[:, W:KCOLS], src[:, :]).then_inc(item_out, 1)
                    return
                dve.wait_ge(item_hi, g * (2 * NH) + half * NH + HI_COUNT[i])
                if kind == "k":
                    nc.vector.tensor_tensor(kT[1][:, b, W:KCOLS], src[:, :], F(kT[0])[:, b, W:KCOLS],
                                            ALU.subtract).then_inc(item_out, 1)
                elif kind == "q":
                    nc.vector.tensor_tensor(qT[1][:, b, :, n, :], src[:, :].rearrange("p (j q) -> p j q", j=NJ),
                                            F(qT[0])[:, b, :, n, :], ALU.subtract).then_inc(item_out, 1)
                else:
                    at = slice(b * NJ + 4 * n, b * NJ + 4 * n + 4)
                    nc.vector.tensor_tensor(v[1][:, at, :], src[:, :].rearrange("p (j d) -> p j d", j=4),
                                            F(v[0])[:, at, :], ALU.subtract).then_inc(item_out, 1)

            for t in range(T):
                dve.wait_ge(x_in[t], 16)
                nc.vector.bn_stats(stats[:, t, :], acc[:, t, :]).then_inc(dve_chain, 1)
                chain[0] += 1
            dve.wait_ge(dve_chain, chain[0])
            for t in range(T):
                last_ins = nc.vector.bn_aggr(mv[:, t, :], stats[:, t, :])
            link(last_ins)
            nc.vector.tensor_scalar(ve[:, :], mv[:, :, 1], EPS, None, ALU.add).then_inc(ln_var, 1)
            dve.wait_ge(ln_sd, 1)
            link(nc.vector.reciprocal(rs[:, :], sd[:, :]))
            link(nc.vector.tensor_tensor(tmp[:, :], rs[:, :], rs[:, :], ALU.mult))
            link(nc.vector.tensor_tensor(tmp[:, :], tmp[:, :], ve[:, :], ALU.mult))
            link(nc.vector.tensor_scalar(tmp[:, :], tmp[:, :], -0.5, 1.5, ALU.mult, ALU.add))
            link(nc.vector.tensor_tensor(rs[:, :], rs[:, :], tmp[:, :], ALU.mult))

            def xlo(t):
                dve.wait_ge(ln_hi, t + 1)
                at = slice(t * P, (t + 1) * P)
                nc.vector.tensor_tensor(xT[1][:, :, at], p_ln[t % 2][:, :].rearrange("p (k c) -> p k c", k=KC),
                                        F(xT[0])[:, :, at], ALU.subtract).then_inc(ln_lo, 1)

            for t in range(T):
                if t >= 4:
                    dve.wait_ge(ln_t, t - 3)
                    dve.wait_ge(xn_kept[t % 4], 16)
                nc.vector.tensor_scalar(ring[:, t % 4, :], acc[:, t, :], mv[:, t, 0:1], rs[:, t:t + 1],
                                        ALU.subtract, ALU.mult).then_inc(ln_xn, 1)
                if t >= 1:
                    xlo(t - 1)
            xlo(T - 1)

            item(0, 0, 0)
            dve.wait_ge(lg_mm, 1)
            dve.wait_ge(small_in, 32)
            nc.vector.tensor_tensor(lg[:, :, :], p_y[:, 0:T * E].rearrange("p (t e) -> p t e", t=T),
                                    bg_b[:, :].unsqueeze(1).to_broadcast([P, T, E]), ALU.add).then_inc(lg_read, 1)
            dve.wait_ge(lg_read, 1)
            for t in range(T):
                last_ins = nc.vector.max(top[:, t, :], lg[:, t, :])
            link(last_ins)
            for t in range(T):
                last_ins = nc.vector.max_index(topi[:, t, :], top[:, t, :], lg[:, t, :])
            link(last_ins)
            item(0, 0, 1)
            link(nc.vector.tensor_copy(topf[:, :, :], topi[:, :, 0:2]))
            dve.wait_ge(consts, 1)
            for s in range(4):
                dve.wait_ge(xn_kept[s], 16 * (T // 4))
            dve.wait_ge(ln_t, T)
            n_tk = 2 * T

            def over(a, n, m):
                return a.unsqueeze(2).to_broadcast([P, n, m])

            def row(a, n, m):
                return a.unsqueeze(1).to_broadcast([P, n, m])

            link(nc.vector.tensor_tensor(is_top, row(iota_e[:, :], n_tk, E),
                                         over(topf[:, :, :].rearrange("p t k -> p (t k)"), n_tk, E), ALU.is_equal))
            by_k = is_top.rearrange("p (t k) e -> p t k e", k=2)
            nc.vector.tensor_tensor(member[:, :, :], by_k[:, :, 0, :], by_k[:, :, 1, :],
                                    ALU.add).then_inc(member_done, 1)
            item(0, 0, 2)
            dve.wait_ge(rank_mm, 1)
            ahead = p_out[:, 0:T * E].rearrange("p (t o e) -> p t o e", t=T, o=1).to_broadcast([P, T, 2, E])
            nc.vector.tensor_tensor(prod.rearrange("p (t k) e -> p t k e", k=2), by_k, ahead, ALU.mult)
            link(nc.vector.tensor_tensor(cmp_n, over(p_out[:, T * E:T * E + E], E, 8), row(steps[:, :], E, 8), ALU.is_gt))
            nc.vector.tensor_reduce(rank[:, :], prod, AX.X, ALU.add)
            link(nc.vector.tensor_reduce(tiles_e[:, :], cmp_n, AX.X, ALU.add))
            item(0, 0, 3)
            link(nc.vector.tensor_tensor(prod_e, before[:, :, :], row(tiles_e[:, :], E, E), ALU.mult))
            link(nc.vector.tensor_reduce(tile0[:, :], prod_e, AX.X, ALU.add))
            nc.vector.tensor_tensor(cmp_q, over(rank[:, :], n_tk, 7), row(steps[:, 1:8], n_tk, 7), ALU.is_ge)
            nc.vector.tensor_tensor(prod2, is_top, row(tile0[:, :], n_tk, E), ALU.mult)
            link(nc.vector.tensor_tensor(tile1[:, :], tile0[:, :], tiles_e[:, :], ALU.add))
            nc.vector.tensor_tensor(cmp_t, over(iota_t[:, :], MT, E), row(tile1[:, :], MT, E), ALU.is_ge)
            nc.vector.tensor_reduce(rtile[:, :], prod2, AX.X, ALU.add)
            link(nc.vector.tensor_reduce(rfull[:, :], cmp_q, AX.X, ALU.add))
            item(0, 0, 4)
            nc.vector.tensor_reduce(expert_f[:, :], cmp_t, AX.X, ALU.add)
            link(nc.vector.scalar_tensor_tensor(rpos[:, :], rank[:, :], float(MT), rtile[:, :], ALU.mult, ALU.add))
            nc.vector.tensor_scalar(expert[:, :], expert_f[:, :], float(E - 1), None, ALU.min)
            nc.vector.scalar_tensor_tensor(slot[:, :], rfull[:, :], float(1 - MT * P), rpos[:, :],
                                           ALU.mult, ALU.add).then_inc(routed, 1)
            for i in range(5, NI):
                item(0, 0, i)

            def a_pass(g, last):
                for s in range(STEPS):
                    if s < T:
                        dve.wait_ge(s_mm, unit(g, s + 1))
                        for jj in range(2):
                            kind = 0 if s % TB == 0 and jj == 0 else 1
                            half = p_s[s % 2][:, jj * 256:jj * 256 + 256].rearrange("p (c n) -> p c n", c=2)
                            ins = nc.vector.scalar_tensor_tensor(
                                half, half, SCALE, mask[:, kind:kind + 1, :].to_broadcast([P, 2, P]),
                                ALU.mult, ALU.add)
                        ins.then_inc(s_read, 1)
                        dve.wait_ge(s_read, unit(g, s + 1))
                        nc.vector.tensor_reduce(nmax[:, s % 2, :], p_s[s % 2][:, :].rearrange("p (c n) -> p c n", c=4),
                                                AX.X, ALU.max, negate=True).then_inc(s_max, 1)
                    mine = items_in(s, last)
                    for half, i in mine[:1]:
                        item(g, half, i)
                    if s < T:
                        dve.wait_ge(p_exp, unit(g, s + 1))
                        nc.vector.reciprocal(rinv[:, :], rsum[:, s % 2, :]).then_inc(p_inv, 1)
                        dve.wait_ge(p_inv, unit(g, s + 1))
                        nc.vector.tensor_tensor(pr[:, s % 2, :, :], pr[:, s % 2, :, :], over(rinv[:, :], 4, P),
                                                ALU.mult).then_inc(p_norm, 1)
                    for half, i in mine[1:]:
                        item(g, half, i)
                    if s in X_STEP:
                        dve.wait_ge(x_hi, tile(g, X_STEP[s]) + 1)
                        nc.vector.tensor_tensor(xgT[1][:, :, :].rearrange("p k c -> p (k c)"), p_y[:, :],
                                                F(xgT[0])[:, :, :].rearrange("p k c -> p (k c)"),
                                                ALU.subtract).then_inc(x_lo, 1)
                    if s in Y_STEP:
                        c = Y_STEP[s]
                        dve.wait_ge(y_mm, tile(g, c) + 1)
                        dve.wait_ge(be_in, g * (16 * MP) + 16 * (c + 1))
                        nc.vector.tensor_tensor(p_y[:, :], p_y[:, :], be_b[:, :], ALU.add).then_inc(y_bias, 1)
                    if 1 <= s <= T:
                        dve.wait_ge(pt_hi, unit(g, s))
                        nc.vector.tensor_tensor(pT[1][:, :, :, :].rearrange("p j h q -> p (j h q)"), p_pt[:, :],
                                                F(pT[0])[:, :, :, :].rearrange("p j h q -> p (j h q)"),
                                                ALU.subtract).then_inc(pt_lo, 1)
                    if s >= 2:
                        u = s - 2
                        dve.wait_ge(out_mm, unit(g, u + 1))
                        nc.vector.tensor_tensor(acc[:, u, :], p_out[:, :], acc[:, u, :], ALU.add).then_inc(out_acc, 1)
                    if 1 <= s <= T:
                        dve.wait_ge(o_hi, unit(g, s))
                        nc.vector.tensor_tensor(oT[1][:, :, :].rearrange("p h (j q) -> p j h q", j=2),
                                                p_o[:, :].rearrange("p (j h q) -> p j h q", j=2, h=HG),
                                                F(oT[0])[:, :, :].rearrange("p h (j q) -> p j h q", j=2),
                                                ALU.subtract).then_inc(o_lo, 1)

            with dve.Fori(0, G - 1) as g:
                a_pass(g, False)
            a_pass(G - 1, True)
            for t in range(T):
                dve.wait_ge(x_in[t], 32)
                dve.wait_ge(out_acc, unit(G - 1, t + 1))
                nc.vector.tensor_tensor(acc[:, t, :], acc[:, t, :], y_in[:, t, :], ALU.add).then_inc(summed, 1)

        @block.tensor
        def _(pe):
            for signal in (s_mm, pt_mm, o_mm, out_mm, x_mm, y_mm):
                pe.sem_inc(signal, FREE)

            def product(out_ap, terms):
                n = 0
                for (ah, al), (bh, bl) in terms:
                    for a, b in ((ah, bh), (ah, bl), (al, bh)):
                        n += 1
                        ins = nc.tensor.matmul(out_ap, a, b, start=(n == 1), stop=(n == 3 * len(terms)))
                return ins

            def cut(halves, *index):
                return halves[0][index], halves[1][index]

            A = slice(None)

            def item(g, half, i, last=False):
                kind, n = ITEM[i]
                b = half % 2
                dst = p_item[i % 2]
                if i == 0 and half != 1:
                    pe.wait_ge(w_split, 1 if half == 0 else split_count(g, "kv"))
                if i == 2 and half != 1:
                    pe.wait_ge(w_split, NF if half == 0 else split_count(g, "q1"))
                if half != 0 or i >= 2:
                    pe.wait_ge(item_out, nth(g, half, i - 1))
                if kind == "t":
                    for c in range(4):
                        j = n * 4 + c
                        ins = nc.tensor.transpose(dst[:, c * P:(c + 1) * P], vT[:, j * W:j * W + P], ident[:, :])
                else:
                    w, m = {"k": (w_kv, 0), "v": (w_kv, 1), "q": (w_q, n)}[kind]
                    ins = product(dst[:, :], [(cut(w, A, m, k, A), cut(xT, A, k, slice(b * NTOK, (b + 1) * NTOK)))
                                              for k in range(KC)])
                ins.then_inc(item_mm, 1)

            pe.wait_ge(cleared, 1)
            for t in range(T):
                pe.wait_ge(ln_xn, t + 1)
                if t >= 2:
                    pe.wait_ge(ln_lo, t - 1)
                for k in range(KC):
                    ins = nc.tensor.transpose(p_ln[t % 2][:, k * P:(k + 1) * P], ring[:, t % 4, k * P:(k + 1) * P],
                                              ident[:, :])
                ins.then_inc(ln_t, 1)
            pe.wait_ge(wg_done, 1)
            for h in range(2):
                pe.wait_ge(ln_lo, TB * (h + 1))
                for k in range(KC):
                    for n, a in enumerate(xT):
                        ins = nc.tensor.matmul(p_s[h][:, :], xgT[0][:, k, :], a[:, k, h * 512:(h + 1) * 512],
                                               start=(k + n == 0), stop=(k + n == KC))
                ins.then_inc(lgT_mm, 1)
            item(0, 0, 0)
            pe.wait_ge(lgT_out, 2)
            for t in range(T):
                ins = nc.tensor.matmul(p_y[:, t * E:(t + 1) * E], lgT[:, t * P:(t + 1) * P], fold[:, :],
                                       start=True, stop=True)
            ins.then_inc(lg_mm, 1)
            item(0, 0, 1)
            item(0, 0, 2)
            pe.wait_ge(member_done, 1)
            for t in range(T - 1):
                n = T - 1 - t
                nc.tensor.matmul(p_out[:, (t + 1) * E:T * E], ones[:, :],
                                 member[:, t:t + 1, :].to_broadcast([P, n, E]), start=(t == 0), stop=False,
                                 skip_group_check=True)
            nc.tensor.matmul(p_out[:, 0:T * E], below[:, :], member[:, :, :].rearrange("p t e -> p (t e)"),
                             start=False, stop=True, skip_group_check=True)
            for t in range(T):
                ins = nc.tensor.matmul(p_out[:, T * E:T * E + E], ones[:, :], member[:, t, :],
                                       start=(t == 0), stop=(t == T - 1), skip_group_check=True)
            ins.then_inc(rank_mm, 1)
            for i in range(3, NI):
                item(0, 0, i)

            def a_pass(g, last):
                for s in range(STEPS):
                    if s < T:
                        b, t = divmod(s, TB)
                        pe.wait_ge(item_out, nth(g, 1 + b, 0))
                        pe.wait_ge(p_exp, unit(g, max(s - 1, 0)))
                        if s == 0:
                            pe.wait_ge(consts, 1)
                        for c in range(4):
                            j, hp = 2 * t + c // 2, c % 2
                            ins = product(p_s[s % 2][:, c * P:(c + 1) * P],
                                          [(cut(qT, A, b, j, slice(2 * hp, 2 * hp + 2), A),
                                            cut(kT, A, b, slice(j * W, j * W + P)))])
                        ins.then_inc(s_mm, 1)
                    for half, i in items_in(s, last):
                        item(g, half, i)
                    if s in X_STEP:
                        c = X_STEP[s]
                        buf = XG_BUF[c]
                        per = XG_BUF.count(buf)
                        pe.wait_ge(xg_in[buf], g * (16 * per) + 16 * (XG_BUF[:c].count(buf) + 1))
                        pe.wait_ge(y_relu, tile(g, c))
                        for k in range(KC):
                            ins = nc.tensor.transpose(p_y[:, k * P:(k + 1) * P], xg[:, buf, k * P:(k + 1) * P],
                                                      ident[:, :])
                        ins.then_inc(x_mm, 1)
                    if s in Y_STEP:
                        c = Y_STEP[s]
                        pe.wait_ge(w_split, split_count(g, f"e{c}b", last))
                        pe.wait_ge(x_lo, tile(g, c) + 1)
                        product(p_y[:, :], [(cut(xgT, A, k, A), cut(w_e, A, k, A)) for k in range(KC)]).then_inc(y_mm, 1)
                    if 1 <= s <= T:
                        u = s - 1
                        pe.wait_ge(p_norm, unit(g, u + 1))
                        pe.wait_ge(pt_lo, unit(g, u))
                        for c in range(4):
                            ins = nc.tensor.transpose(p_pt[:, c * P:(c + 1) * P], pr[:, u % 2, c, :], ident[:, :])
                        ins.then_inc(pt_mm, 1)
                    if s >= 2:
                        u = s - 2
                        if u == 0:
                            pe.wait_ge(w_split, split_count(g, "o1", last))
                        pe.wait_ge(o_lo, unit(g, u + 1))
                        pe.wait_ge(out_acc, unit(g, u))
                        product(p_out[:, :], [(cut(oT, A, h, A), cut(w_o, A, h, A)) for h in range(HG)]
                                ).then_inc(out_mm, 1)
                    if 1 <= s <= T:
                        u = s - 1
                        b, t = divmod(u, TB)
                        pe.wait_ge(pt_lo, unit(g, u + 1))
                        pe.wait_ge(o_lo, unit(g, u))
                        for jj in range(2):
                            ins = product(p_o[:, jj * 256:(jj + 1) * 256],
                                          [(cut(v, A, b * NJ + 2 * t + jj, A), cut(pT, A, jj, A, A))])
                        ins.then_inc(o_mm, 1)

            with pe.Fori(0, G - 1) as g:
                a_pass(g, False)
            a_pass(G - 1, True)


def kernel(**inputs):
    import numpy as np
    import concourse.bacc as bacc
    from concourse.bass_utils import run_bass_kernel_spmd as run

    def arr(name):
        return np.asarray(inputs[name])

    def heads(w, n):
        return np.ascontiguousarray(w.reshape(G, n, HD, KC, P).transpose(0, 4, 1, 3, 2).reshape(G, P, n * KC * HD))

    a = {
        "x": np.ascontiguousarray(arr("L0_attn_x").reshape(ROWS, DM)),
        "wq": heads(arr("L0_attn_wq"), HG),
        "wkv": np.concatenate([heads(arr("L0_attn_wk"), 1), heads(arr("L0_attn_wv"), 1)], axis=2),
        "wo": np.ascontiguousarray(arr("L0_attn_wo").reshape(DM, G, HG, HD).transpose(1, 3, 2, 0)
                                   .reshape(G, HD, HG * DM)),
        "wg": np.ascontiguousarray(arr("L0_ffn_W_gate")),
        "bg": np.ascontiguousarray(arr("L0_ffn_b_gate")),
        "we": np.ascontiguousarray(arr("L0_ffn_W_e").reshape(E, KC, P, DM).transpose(0, 2, 1, 3)
                                   .reshape(E, P, KC * DM)),
        "be": np.ascontiguousarray(arr("L0_ffn_b_e")),
    }
    nc = bacc.Bacc("TRN2", target_bir_lowering=False, num_devices=1)
    args = [nc.dram_tensor(f"in_{n}", v.shape, mybir.dt.from_np(v.dtype), kind="ExternalInput").ap()
            for n, v in a.items()]
    args.append(nc.dram_tensor("out_0", (ROWS, DM), mybir.dt.float32, kind="ExternalOutput").ap())
    build(nc, *args)
    r = run(nc, [{f"in_{n}": v for n, v in a.items()}], core_ids=[0])
    return r.results[0]["out_0"].reshape(NB, NTOK, DM)
```

```python
import concourse.bass as bass
from concourse import mybir
from contextlib import ExitStack

P = 128
NB, NTOK, DM = 2, 512, 512
ROWS = NB * NTOK
T = ROWS // P
TB = NTOK // P
KC = DM // P
HD = 128
HG = 4
G = 8
E = 8
W = 64
NJ = NTOK // W
KCOLS = W + NTOK
MT = 2 * ROWS // P + E - 1
MP = -(-MT // G)
ML = MT - (G - 1) * MP
NEG = -3.0e38
EPS = 1e-5

ITEM = [("k", 0), ("v", 0), ("t", 0), ("q", 0), ("q", 1), ("q", 2), ("q", 3)]
NI = len(ITEM)
HI_COUNT = [sum(k != "v" for k, _ in ITEM[:i + 1]) for i in range(NI)]
NH = HI_COUNT[-1]
STEPS = T + 2
ITEMS = {0: [(1, 2), (1, 3)], 1: [(1, 4), (1, 5)], 3: [(1, 6)],
         5: [(2, 0), (2, 1)], 6: [(2, 2), (2, 3)], 7: [(2, 4)], 8: [(2, 5), (2, 6)], 9: [(3, 0), (3, 1)]}
ITEM_AHEAD = (0, 1)
OUT_AHEAD = (0, 1)
X_EARLY = (1,)
Y_AHEAD = (2,)
X_STEP = {1: 0, 3: 1, 5: 2}
Y_STEP = {2: 0, 4: 1, 7: 2}
XG_BUF = [0, 1, 0]
CHUNKS = ["e0a", "e0b", "o0", "o1", "e1a", "e1b", "kv", "q0", "q1", "e2a", "e2b"]
SLOT = {"e0a": 0, "e0b": 1, "o0": 2, "o1": 3, "e1a": 0, "e1b": 1, "kv": 2, "q0": 3, "q1": 0, "e2a": 1, "e2b": 2}
FIRST = ["kv", "q0", "q1"]
NC, NF = len(CHUNKS), len(FIRST)
SUM_FIRST = [6, 7]
WARM = 40
FREE = 1


def chunks_of(last):
    return [c for c in CHUNKS if not (last and (c in FIRST or c in ("e2a", "e2b")))]


def tile_at(steps, step, last):
    c = steps.get(step)
    return None if c is None or (last and c >= ML) else c


def split_count(g, name, last=False):
    return NF + g * NC + chunks_of(last).index(name) + 1


def arrived(g, name, last=False):
    slot = SLOT[name]
    ahead = sum(SLOT[c] == slot for c in FIRST)
    a_pass = sum(SLOT[c] == slot for c in CHUNKS)
    order = chunks_of(last)
    return 16 * ahead + g * (16 * a_pass) + 16 * sum(SLOT[c] == slot for c in order[:order.index(name) + 1])


def build(nc, x, wq, wkv, wo, wg, bg, we, be, out):
    fp32, f32r, bf16 = mybir.dt.float32, mybir.dt.float32r, mybir.dt.bfloat16
    u32, i32 = mybir.dt.uint32, mybir.dt.int32
    ALU = mybir.AluOpType
    ACT = mybir.ActivationFunctionType
    AX = mybir.AxisListType
    SCALE = float(HD) ** -0.5

    xn_rows = nc.dram_tensor("xn_rows", (ROWS + P, DM), fp32, kind="Internal").ap()
    y_rows = nc.dram_tensor("y_rows", (ROWS + P, DM), fp32, kind="Internal").ap()
    NZ = 3

    ctx = ExitStack()
    with ctx:
        def sb(name, shape, dt=fp32):
            return ctx.enter_context(nc.sbuf_tensor(name, shape, dt))

        def pair(name, shape):
            return sb(name + "_hi", shape, f32r), sb(name + "_lo", shape, f32r)

        def sem(name):
            return ctx.enter_context(nc.semaphore(name))

        xT = pair("xT", [P, KC, ROWS])
        w_kv = pair("w_kv", [P, 2, KC, P])
        w_q = pair("w_q", [P, HG, KC, P])
        w_o = pair("w_o", [P, HG, DM])
        w_e = pair("w_e", [P, KC, DM])
        stage = sb("stage", [P, 4, 1024])
        kT_both = sb("kT", [P, 2, NB, KCOLS], f32r)
        kT = kT_both[:, 0, :, :], kT_both[:, 1, :, :]
        vT = sb("vT", [P, NTOK])
        v_both = sb("v", [P, NB, 2, TB, 2, HD], f32r)
        v = v_both[:, :, 0, :, :, :], v_both[:, :, 1, :, :, :]
        qT = pair("qT", [P, NB, NJ, HG, W])
        ring = sb("ring", [P, 4, DM])
        pr = ring[:, 0:2, :].rearrange("p b (c n) -> p b c n", c=4)
        xg = ring[:, 2:4, :]
        pT = pair("pT", [P, 2, HG, W])
        oT = pair("oT", [P, HG, P])
        xgT = pair("xgT", [P, KC, P])
        acc = sb("acc", [P, T, DM])
        y = sb("y", [P, DM])
        be_b = sb("be_b", [P, DM])
        ident = sb("ident", [P, P])
        mask = sb("mask", [P, 2, P])
        nmax = sb("nmax", [P, 2, 4])
        rsum = sb("rsum", [P, 2, 4])
        rinv = sb("rinv", [P, 4])
        carry = sb("carry", [P, 3 * MP + 1])
        stats = be_b[:, 192:240].rearrange("p (t n) -> p t n", n=6)
        mv = sb("mv", [P, T, 2])
        ve, sd, rs, tmp = (sb(n, [P, T]) for n in ("ve", "sd", "rs", "tmp"))
        wg_f = be_b[:, 320:352].rearrange("p (k e) -> p k e", e=E)
        bg_b = sb("bg_b", [P, E])
        fold = sb("fold", [P, E])
        below = sb("below", [P, P], bf16)
        ones = sb("ones", [P, P], bf16)
        member = sb("member", [P, T, E], bf16)
        iota_e = sb("iota_e", [P, E])
        iota_t = sb("iota_t", [P, MT])
        steps = sb("steps", [P, 8])
        before = be_b[:, 256:320].rearrange("p (e f) -> p e f", f=E)
        lg = be_b[:, 0:64].rearrange("p (t e) -> p t e", e=E)
        top = be_b[:, 64:128].rearrange("p (t n) -> p t n", n=8)
        topi = be_b[:, 128:192].bitcast(u32).rearrange("p (t n) -> p t n", n=8)
        topf = sb("topf", [P, T, 2])
        tiles_e, tile0, tile1 = (sb(n, [P, E]) for n in ("tiles_e", "tile0", "tile1"))
        expert_f = sb("expert_f", [P, MT])
        expert = sb("expert", [P, MT], i32)
        rank, rtile, rfull, pos, in_tile, off = (sb(n, [P, 2 * T]) for n in
                                                 ("rank", "rtile", "rfull", "pos", "in_tile", "off"))
        base_t = sb("base_t", [P, 2 * T])
        lane = sb("lane", [P, 1])
        lane_rows = sb("lane_rows", [P, 1])
        slot_token = sb("slot_token", [P, MT], u32)
        idx = [sb(f"idx{c}", [P, 1], u32) for c in range(MP)]
        scratch = ring[:, :, :].rearrange("p b n -> p (b n)")
        is_top = scratch[:, 0:128].rearrange("p (a e) -> p a e", e=E)
        prod = scratch[:, 128:256].rearrange("p (a e) -> p a e", e=E)
        cmp_q = scratch[:, 256:368].rearrange("p (a j) -> p a j", j=7)
        cmp_n = scratch[:, 384:448].rearrange("p (e j) -> p e j", j=8)
        prod_e = scratch[:, 448:512].rearrange("p (e f) -> p e f", f=E)
        cmp_t = scratch[:, 512:512 + MT * E].rearrange("p (i e) -> p i e", e=E)
        prod2 = scratch[:, 704:832].rearrange("p (a e) -> p a e", e=E)
        is_tile = scratch[:, 1024:1024 + 2 * T * MT].rearrange("p (a i) -> p a i", i=MT)
        row_parts = scratch[:, 1408:1408 + 2 * T * MT].bitcast(bf16).rearrange("p (a h i) -> p a h i", h=2, i=MT)
        iota_p = be_b[:, 352:352 + P]
        is_lane = stage[:, SLOT["o1"], :].bitcast(bf16).rearrange("p (a n) -> p a n", n=P)
        lgT = stage[:, SLOT["o1"], :]
        y_in = stage[:, :, :].rearrange("p s (t n) -> p (s t) n", n=DM)

        def bank(name):
            return ctx.enter_context(nc.psum_tensor(name, [P, 512], fp32))
        p_item = [bank("p_item0"), bank("p_item1")]
        p_scores = ctx.enter_context(nc.psum_tensor("p_scores", [P, 4, 2, P], fp32))
        p_main, p_small = p_scores[:, :, 0, :], p_scores[:, :, 1, :]
        p_logit = [p_scores[:, 2 * h:2 * h + 2, :, :].rearrange("p a b n -> p (a b n)") for h in range(2)]
        p_pt, p_o, p_out, p_y = bank("p_pt"), bank("p_o"), bank("p_out"), bank("p_y")
        p_ln = [p_pt, p_o, p_y, p_out]

        x_in = [sem(f"x_in{i}") for i in range(T)]
        small_in = sem("small_in")
        w_in = [sem(f"w_in{i}") for i in range(4)]
        w_hi, w_split = sem("w_hi"), sem("w_split")
        be_in = sem("be_in")
        consts, wg_done, pool_chain, dve_chain = sem("consts"), sem("wg_done"), sem("pool_chain"), sem("dve_chain")
        ident_made = sem("ident_made")
        cleared = sem("cleared")
        ln_var, ln_sd, ln_xn = sem("ln_var"), sem("ln_sd"), sem("ln_xn")
        ln_t, ln_hi, ln_lo = sem("ln_t"), sem("ln_hi"), sem("ln_lo")
        xn_kept = [sem(f"xn_kept{i}") for i in range(4)]
        pad_kept = sem("pad_kept")
        lgT_mm, lgT_out, lg_mm, lg_read = sem("lgT_mm"), sem("lgT_out"), sem("lg_mm"), sem("lg_read")
        member_done, rank_mm, routed = sem("member_done"), sem("rank_mm"), sem("routed")
        tiles_done, lanes_done, table_mm, table_done = sem("tiles_done"), sem("lanes_done"), sem("table_mm"), sem("table_done")
        v_shifted = sem("v_shifted")
        item_mm, item_hi, item_out = sem("item_mm"), sem("item_hi"), sem("item_out")
        s_mm, s_masked, s_read, s_max = sem("s_mm"), sem("s_masked"), sem("s_read"), sem("s_max")
        p_exp, p_inv, p_norm = sem("p_exp"), sem("p_inv"), sem("p_norm")
        pt_mm, pt_hi, pt_lo = sem("pt_mm"), sem("pt_hi"), sem("pt_lo")
        o_mm, o_hi, o_lo = sem("o_mm"), sem("o_hi"), sem("o_lo")
        out_mm, out_acc = sem("out_mm"), sem("out_acc")
        idx_done = sem("idx_done")
        xg_in = [sem("xg_in0"), sem("xg_in1")]
        x_mm, x_hi, x_lo = sem("x_mm"), sem("x_hi"), sem("x_lo")
        y_mm, y_bias, y_relu = sem("y_mm"), sem("y_bias"), sem("y_relu")
        y_added = sem("y_added")
        summed, stored = sem("summed"), sem("stored")

        def F(a):
            return a.bitcast(fp32)

        def nth(g, half, i):
            return g * (2 * NI) + half * NI + i

        def items_in(step, last):
            return [(half, i) for half, i in ITEMS.get(step, []) if half == 1 or not last]

        def unit(g, u):
            return FREE + g * T + u

        def tile(g, c):
            return FREE + g * MP + c

        block = ctx.enter_context(nc.Block())

        @block.sync
        def _(sp):
            att = {"kv": lambda g: wkv[g, :, :], "q0": lambda g: wq[g, :, 0:1024], "q1": lambda g: wq[g, :, 1024:2048],
                   "o0": lambda g: wo[g, :, 0:1024], "o1": lambda g: wo[g, :, 1024:2048]}
            for t in range(T):
                sp.dma_start(acc[:, t, :], x[t * P:(t + 1) * P, :]).then_inc(x_in[t], 16)
                if t == TB - 1:
                    sp.dma_start(stage[:, SLOT["kv"], :], att["kv"](0)).then_inc(w_in[SLOT["kv"]], 16)
            sp.dma_start(wg_f[:, :, :], wg.rearrange("(k p) e -> p k e", p=P)).then_inc(small_in, 16)
            sp.dma_start(bg_b[:, :], bg.partition_broadcast(P)).then_inc(small_in, 16)
            for c in FIRST[1:]:
                sp.dma_start(stage[:, SLOT[c], :], att[c](0)).then_inc(w_in[SLOT[c]], 16)
            sp.wait_ge(cleared, 1)
            sp.dma_start(xn_rows[ROWS:ROWS + P, :], y[:, :]).then_inc(pad_kept, 16)
            for t in range(T):
                sp.wait_ge(ln_xn, t + 1)
                sp.dma_start(xn_rows[t * P:(t + 1) * P, :], ring[:, t % 4, :]).then_inc(xn_kept[t % 4], 16)

            def shift_v(g, half):
                b = half % 2
                sp.wait_ge(item_out, nth(g, half, 2) + 1)
                blocks = F(v_both)[:, b, :, :, :, :].rearrange("p h c o d -> p (h c) o d")
                sp.dma_start(blocks[W:P, :, 0, :], blocks[0:W, :, 1, :]).then_inc(v_shifted, 16)
                for h in range(2):
                    c = h * TB
                    sp.dma_start(blocks[0:W, c + 1:c + TB, 0, :], blocks[W:P, c:c + TB - 1, 1, :]).then_inc(v_shifted, 16)

            sp.wait_ge(consts, 1)
            shift_v(0, 0)
            sp.wait_ge(routed, 1)

            def a_pass(g, last):
                order = chunks_of(last)
                for n, name in enumerate(order):
                    s = SLOT[name]
                    prev = [c for c in order[:n] if SLOT[c] == s]
                    sp.wait_ge(w_split, split_count(g, prev[-1], last) if prev else NF + g * NC)
                    if name == "o1":
                        sp.wait_ge(table_mm, 1)
                    if name[0] == "e":
                        c, half = int(name[1]), "ab".index(name[2])
                        if half == 0:
                            e = sp.value_load(expert[0:1, bass.ds(g * MP + c, 1)], min_val=0, max_val=E - 1)
                        src = we[bass.ds(e, 1), :, half * 1024:(half + 1) * 1024].rearrange("o p n -> (o p) n")
                        sp.dma_start(stage[:, s, :], src).then_inc(w_in[s], 16)
                        if half == 1:
                            sp.wait_ge(y_bias, tile(g, c))
                            sp.wait_ge(table_mm, 1)
                            sp.dma_start(be_b[:, :], be[bass.ds(e, 1), :].rearrange("o n -> (o n)").partition_broadcast(P)
                                         ).then_inc(be_in, 16)
                    else:
                        sp.dma_start(stage[:, s, :], att[name](g + 1 if name in FIRST else g)).then_inc(w_in[s], 16)
                    if name == "e1a":
                        shift_v(g, 1)
                if not last:
                    shift_v(g, 2)

            with sp.Fori(0, G - 1) as g:
                a_pass(g, False)
            a_pass(G - 1, True)
            sp.wait_ge(y_added, 16 * (NZ + MT))
            sp.wait_ge(w_split, split_count(G - 1, "e1b", True))
            for t in range(T):
                sp.dma_start(y_in[:, t, :], y_rows[t * P:(t + 1) * P, :]).then_inc(x_in[t], 16)
            for t in range(T):
                sp.wait_ge(summed, T if t in SUM_FIRST else len(SUM_FIRST) + t + 1)
                sp.wait_ge(out_acc, unit(G - 1, t + 1))
                sp.dma_start(out[t * P:(t + 1) * P, :], acc[:, t, :]).then_inc(stored, 16)
            sp.wait_ge(stored, 16 * T)

        @block.gpsimd
        def _(pool):
            pool.sem_inc(idx_done, FREE)
            chain = [0]

            def link(ins):
                chain[0] += 1
                ins.then_inc(pool_chain, 1)
                pool.wait_ge(pool_chain, chain[0])

            def select(a, op, fill, base, pattern, mult):
                link(nc.gpsimd.affine_select(out=a, in_=a, compare_op=op, fill=fill, base=base,
                                             pattern=pattern, channel_multiplier=mult))

            def iota(a, pattern, base, mult):
                nc.gpsimd.iota(a, pattern=pattern, base=base, channel_multiplier=mult,
                               allow_small_or_imprecise_dtypes=True)

            link(nc.gpsimd.memset(ident[:, :], 0.0))
            nc.gpsimd.affine_select(out=ident[:, :], in_=ident[:, :], compare_op=ALU.not_equal, fill=1.0, base=0,
                                    pattern=[[-1, P]], channel_multiplier=1).then_inc(ident_made, 1)
            nc.gpsimd.memset(y[:, :], 0.0)
            iota(lane[:, :], [[0, 1]], 0, 1)
            iota(lane_rows[:, :], [[0, 1]], ROWS, 1)
            iota(base_t[:, :], [[P, T], [0, 2]], -ROWS, 0)
            iota(iota_p, [[1, P]], 0, 0)
            link(nc.gpsimd.memset(fold[:, :], 0.0))
            select(fold[:, :], ALU.not_equal, 1.0, 0, [[-1, E]], 1)
            select(fold[:, :], ALU.not_equal, 1.0, -E, [[-1, E]], 1)
            nc.gpsimd.memset(F(xgT[0])[:, :, :], 0.0).then_inc(cleared, 1)
            for b in range(NB):
                nc.gpsimd.memset(F(kT[0])[:, b, 0:W], 0.0)
                nc.gpsimd.memset(F(kT[1])[:, b, 0:W], 0.0)
                nc.gpsimd.memset(F(v_both)[0:W, b, :, 0, 0, :], 0.0)
            iota(iota_e[:, :], [[1, E]], 0, 0)
            iota(iota_t[:, :], [[1, MT]], 0, 0)
            iota(steps[:, :], [[P, 8]], 0, 0)
            link(nc.gpsimd.memset(ones[:, :], 1.0))
            link(nc.gpsimd.memset(below[:, :], 1.0))
            select(below[:, :], ALU.is_gt, 0.0, 0, [[1, P]], -1)
            link(nc.gpsimd.memset(before[:, :, :], 1.0))
            select(before[:, :, :], ALU.is_gt, 0.0, 0, [[1, E], [-1, E]], 0)
            nc.gpsimd.tensor_tensor(carry[:, 0:1], iota_e[:, 0:1], iota_e[:, 0:1], ALU.add).then_inc(consts, 1)
            carried = [0]

            halves = {"kv": [h[:, :, :, :].rearrange("p a k m -> p (a k m)") for h in w_kv]}
            for n in range(2):
                halves[f"q{n}"] = [h[:, 2 * n:2 * n + 2, :, :].rearrange("p a k m -> p (a k m)") for h in w_q]
                halves[f"o{n}"] = [h[:, 2 * n:2 * n + 2, :].rearrange("p k m -> p (k m)") for h in w_o]
                for c in range(MP):
                    halves[f"e{c}{'ab'[n]}"] = [h[:, 2 * n:2 * n + 2, :].rearrange("p k m -> p (k m)") for h in w_e]

            def lo(name, count):
                pool.wait_ge(w_hi, count)
                hi_ap, lo_ap = halves[name]
                nc.gpsimd.tensor_tensor(lo_ap, stage[:, SLOT[name], :], F(hi_ap), ALU.subtract).then_inc(w_split, 1)

            def held():
                carried[0] = carried[0] % (3 * MP) + 1
                n = carried[0]
                nc.gpsimd.tensor_tensor(carry[:, n:n + 1], iota_e[:, 0:1], iota_e[:, 0:1], ALU.add)

            lo("kv", 1)
            pool.wait_ge(cleared, 1)
            pool.wait_ge(small_in, 32)
            link(nc.gpsimd.tensor_copy(xgT[0][:, :, 0:E], wg_f[:, :, :]))
            nc.gpsimd.tensor_tensor(xgT[0][:, :, E:2 * E], wg_f[:, :, :], F(xgT[0])[:, :, 0:E],
                                    ALU.subtract).then_inc(wg_done, 1)
            link(nc.gpsimd.memset(mask[:, :, :], 0.0))
            for half in range(2):
                m = mask[half * W:(half + 1) * W, :, :]
                select(m, ALU.is_gt, NEG, 0, [[0, 2], [1, P]], -1)
                select(m, ALU.is_ge, NEG, W, [[0, 2], [-1, P]], 1)
            link(nc.gpsimd.memset(mask[:, 0, 0:W], NEG))
            lo("q0", 2)
            lo("q1", 3)
            y_parts = y_rows.rearrange("(z n p) d -> z p n d", z=NZ, p=P)
            for z in range(NZ):
                nc.gpsimd.dma_start(y_parts[z, :, :, :], y[:, :].unsqueeze(1).to_broadcast([P, (ROWS + P) // P // NZ, DM])
                                    ).then_inc(y_added, 16)
            pool.wait_ge(tiles_done, 1)
            for n, part in enumerate((base_t, off)):
                nc.gpsimd.tensor_tensor(row_parts[:, :, n, :], is_tile, part[:, :].unsqueeze(2).to_broadcast([P, 2 * T, MT]),
                                        ALU.mult).then_inc(lanes_done, 1)
            pool.wait_ge(y_added, 16 * NZ)
            pool.wait_ge(table_done, 1)
            pool.wait_ge(pad_kept, 16)
            for s in range(4):
                pool.wait_ge(xn_kept[s], 16 * (T // 4))

            def gather(g, c):
                pool.wait_ge(y_added, 16 * (NZ - MP + 1) + g * (16 * MP) + 16 * c)
                pool.wait_ge(x_mm, tile(g, 0) if c < 2 else tile(g, 1))
                held()
                nc.gpsimd.tensor_copy(idx[c][:, :], slot_token[:, bass.ds(g * MP + c, 1)]).then_inc(idx_done, 1)
                pool.wait_ge(idx_done, tile(g, c) + 1)
                held()
                nc.gpsimd.indirect_dma_start(xg[:, XG_BUF[c], :], None, xn_rows,
                                             bass.IndirectOffsetOnAxis(ap=idx[c][:, 0:1], axis=0)
                                             ).then_inc(xg_in[XG_BUF[c]], 16)

            def add(g, c):
                pool.wait_ge(y_relu, tile(g, c) + 1)
                pool.wait_ge(y_added, 16 * NZ + g * (16 * MP) + 16 * c)
                held()
                nc.gpsimd.indirect_dma_start(y_rows, bass.IndirectOffsetOnAxis(ap=idx[c][:, 0:1], axis=0),
                                             y[:, :], None, compute_op=ALU.add).then_inc(y_added, 16)

            def a_pass(g, last):
                gather(g, 0)
                gather(g, 1)
                for name in ("e0a", "e0b", "o0", "o1"):
                    lo(name, split_count(g, name, last))
                add(g, 0)
                for name in ("e1a", "e1b"):
                    lo(name, split_count(g, name, last))
                if not last:
                    gather(g, 2)
                if not last:
                    for name in FIRST:
                        lo(name, split_count(g, name))
                add(g, 1)
                if not last:
                    for name in ("e2a", "e2b"):
                        lo(name, split_count(g, name, last))
                    add(g, 2)

            with pool.Fori(0, G - 1) as g:
                a_pass(g, False)
            a_pass(G - 1, True)
            for t in SUM_FIRST + [t for t in range(T) if t not in SUM_FIRST]:
                pool.wait_ge(x_in[t], 32)
                pool.wait_ge(out_acc, unit(G - 2, t + 1) if t in SUM_FIRST else unit(G - 1, t + 1))
                nc.gpsimd.tensor_tensor(acc[:, t, :], acc[:, t, :], y_in[:, t, :], ALU.add).then_inc(summed, 1)

        @block.scalar
        def _(act):
            for signal in (p_exp, pt_hi, o_hi, x_hi, y_relu):
                act.sem_inc(signal, FREE)
            hi_of = {"kv": w_kv[0][:, :, :, :].rearrange("p a k m -> p (a k m)")}
            for n in range(2):
                hi_of[f"q{n}"] = w_q[0][:, 2 * n:2 * n + 2, :, :].rearrange("p a k m -> p (a k m)")
                hi_of[f"o{n}"] = w_o[0][:, 2 * n:2 * n + 2, :].rearrange("p k m -> p (k m)")
                for c in range(MP):
                    hi_of[f"e{c}{'ab'[n]}"] = w_e[0][:, 2 * n:2 * n + 2, :].rearrange("p k m -> p (k m)")

            def hi(name, count):
                act.wait_ge(w_in[SLOT[name]], count)
                nc.scalar.copy(hi_of[name], stage[:, SLOT[name], :]).then_inc(w_hi, 1)

            def item(g, half, i):
                kind, n = ITEM[i]
                if kind == "v":
                    return
                b = half % 2
                act.wait_ge(item_mm, nth(g, half, i) + 1)
                src = p_item[(half * NI + i) % 2]
                if kind == "k":
                    nc.scalar.copy(kT[0][:, b, W:KCOLS], src[:, :]).then_inc(item_hi, 1)
                elif kind == "q":
                    nc.scalar.copy(qT[0][:, b, :, n, :],
                                   src[:, :].rearrange("p (j q) -> p j q", j=NJ)).then_inc(item_hi, 1)
                else:
                    nc.scalar.copy(v[0][:, b, :, 1, :],
                                   src[:, :].rearrange("p (j d) -> p j d", j=4)).then_inc(item_hi, 1)

            def root(half):
                act.wait_ge(ln_var, half + 1)
                at = slice(half * TB, (half + 1) * TB)
                nc.scalar.activation(sd[:, at], ve[:, at], ACT.Sqrt).then_inc(ln_sd, 1)

            def x_hi_half(t):
                act.wait_ge(ln_t, t + 1)
                nc.scalar.copy(xT[0][:, :, t * P:(t + 1) * P],
                               p_ln[t % 4][:, :].rearrange("p (k c) -> p k c", k=KC)).then_inc(ln_hi, 1)

            root(0)
            hi("kv", 16)
            for t in range(TB):
                x_hi_half(t)
            hi("q0", 16)
            hi("q1", 16)
            root(1)
            item(0, 0, 0)
            x_hi_half(4)
            x_hi_half(5)
            item(0, 0, 2)
            item(0, 0, 3)
            x_hi_half(6)
            x_hi_half(7)

            def logits_out(h):
                act.wait_ge(lgT_mm, h + 1)
                nc.scalar.copy(lgT[:, h * 512:(h + 1) * 512], p_logit[h]).then_inc(lgT_out, 1)

            act.wait_ge(w_split, 2)
            logits_out(0)
            logits_out(1)
            for i in range(4, NI):
                item(0, 0, i)
            item(0, 1, 0)
            item(0, 1, 1)

            def rows_hi(g, s, last):
                if tile_at(X_STEP, s, last) is not None:
                    act.wait_ge(x_mm, tile(g, X_STEP[s]) + 1)
                    nc.scalar.copy(xgT[0][:, :, :].rearrange("p k c -> p (k c)"), p_y[:, :]).then_inc(x_hi, 1)

            def a_pass(g, last):
                for s in range(STEPS):
                    mine = items_in(s, last)
                    ahead = int(s in OUT_AHEAD)
                    for half, i in mine[:ahead]:
                        item(g, half, i)
                    if 1 <= s <= T:
                        act.wait_ge(pt_mm, unit(g, s))
                        nc.scalar.copy(pT[0][:, :, :, :].rearrange("p j h q -> p (j h q)"),
                                       p_pt[:, :]).then_inc(pt_hi, 1)
                    if s in X_EARLY:
                        rows_hi(g, s, last)
                    if s == 0:
                        act.wait_ge(y_mm, tile(g, 0))
                        for name in ("e0a", "e0b"):
                            hi(name, arrived(g, name, last))
                    if s == 1:
                        act.wait_ge(out_mm, unit(g, 0))
                        for name in ("o0", "o1"):
                            hi(name, arrived(g, name, last))
                    if s < T:
                        act.wait_ge(s_max, unit(g, s + 1))
                        for c in range(4):
                            e = nc.scalar.activation(pr[:, s % 2, c, :], pr[:, s % 2, c, :], ACT.Exp,
                                                     bias=nmax[:, s % 2, c:c + 1], scale=1.0,
                                                     accum_out=rsum[:, s % 2, c:c + 1])
                        e.then_inc(p_exp, 1)
                    for half, i in mine[ahead:]:
                        item(g, half, i)
                    if s == 4 and not last:
                        for name in FIRST[1:]:
                            hi(name, arrived(g, name))
                    if s not in X_EARLY:
                        rows_hi(g, s, last)
                    if 1 <= s <= T:
                        act.wait_ge(o_mm, unit(g, s))
                        nc.scalar.copy(oT[0][:, :, :].rearrange("p h (j q) -> p j h q", j=2),
                                       p_o[:, :].rearrange("p (j h q) -> p j h q", j=2, h=HG)).then_inc(o_hi, 1)
                    if tile_at(Y_STEP, s, last) is not None:
                        c = Y_STEP[s]
                        act.wait_ge(y_bias, tile(g, c) + 1)
                        act.wait_ge(y_added, 16 * NZ + g * (16 * MP) + 16 * c)
                        nc.scalar.activation(y[:, :], p_y[:, :], ACT.Relu, scale=0.5).then_inc(y_relu, 1)
                    if s in (2, 4) and tile_at(Y_STEP, {2: 4, 4: 7}[s], last) is not None:
                        act.wait_ge(y_mm, tile(g, s // 2))
                        for name in (f"e{s // 2}a", f"e{s // 2}b"):
                            hi(name, arrived(g, name, last))
                    if s == 3 and not last:
                        act.wait_ge(item_mm, nth(g, 2, 0))
                        hi("kv", arrived(g, "kv"))

            with act.Fori(0, G - 1) as g:
                a_pass(g, False)
            a_pass(G - 1, True)

        @block.vector
        def _(dve):
            for signal in (s_masked, s_read, s_max, p_inv, p_norm, pt_lo, o_lo, out_acc, x_lo, y_bias):
                dve.sem_inc(signal, FREE)
            chain = [0]

            def link(ins):
                chain[0] += 1
                ins.then_inc(dve_chain, 1)
                dve.wait_ge(dve_chain, chain[0])

            def item(g, half, i):
                kind, n = ITEM[i]
                b = half % 2
                src = p_item[(half * NI + i) % 2]
                if kind == "v":
                    dve.wait_ge(item_mm, nth(g, half, i) + 1)
                    nc.vector.tensor_copy(vT[:, :], src[:, :]).then_inc(item_out, 1)
                    return
                dve.wait_ge(item_hi, g * (2 * NH) + half * NH + HI_COUNT[i])
                if kind == "k":
                    nc.vector.tensor_tensor(kT[1][:, b, W:KCOLS], src[:, :], F(kT[0])[:, b, W:KCOLS],
                                            ALU.subtract).then_inc(item_out, 1)
                elif kind == "q":
                    nc.vector.tensor_tensor(qT[1][:, b, :, n, :], src[:, :].rearrange("p (j q) -> p j q", j=NJ),
                                            F(qT[0])[:, b, :, n, :], ALU.subtract).then_inc(item_out, 1)
                else:
                    nc.vector.tensor_tensor(v[1][:, b, :, 1, :], src[:, :].rearrange("p (j d) -> p j d", j=4),
                                            F(v[0])[:, b, :, 1, :], ALU.subtract).then_inc(item_out, 1)

            def statistics(half):
                at = slice(half * TB, (half + 1) * TB)
                for t in range(half * TB, (half + 1) * TB):
                    dve.wait_ge(x_in[t], 16)
                    nc.vector.bn_stats(stats[:, t, :], acc[:, t, :]).then_inc(dve_chain, 1)
                    chain[0] += 1
                dve.wait_ge(dve_chain, chain[0])
                for t in range(half * TB, (half + 1) * TB):
                    ins = nc.vector.bn_aggr(mv[:, t, :], stats[:, t, :])
                link(ins)
                nc.vector.tensor_scalar(ve[:, at], mv[:, at, 1], EPS, None, ALU.add).then_inc(ln_var, 1)
                dve.wait_ge(ln_var, half + 1)
                dve.wait_ge(ln_sd, half + 1)
                link(nc.vector.reciprocal(rs[:, at], sd[:, at]))
                link(nc.vector.scalar_tensor_tensor(tmp[:, at], rs[:, at], -0.5, ve[:, at], ALU.mult, ALU.mult))
                link(nc.vector.tensor_tensor(tmp[:, at], tmp[:, at], rs[:, at], ALU.mult))
                link(nc.vector.scalar_tensor_tensor(rs[:, at], tmp[:, at], 1.5, rs[:, at], ALU.add, ALU.mult))

            def xn(t):
                if t >= 4:
                    dve.wait_ge(ln_t, t - 3)
                    dve.wait_ge(xn_kept[t % 4], 16)
                nc.vector.tensor_scalar(ring[:, t % 4, :], acc[:, t, :], mv[:, t, 0:1], rs[:, t:t + 1],
                                        ALU.subtract, ALU.mult).then_inc(ln_xn, 1)

            def xlo(t):
                dve.wait_ge(ln_hi, t + 1)
                at = slice(t * P, (t + 1) * P)
                nc.vector.tensor_tensor(xT[1][:, :, at], p_ln[t % 4][:, :].rearrange("p (k c) -> p k c", k=KC),
                                        F(xT[0])[:, :, at], ALU.subtract).then_inc(ln_lo, 1)

            statistics(0)
            for t in range(TB):
                xn(t)
            for t in range(TB):
                xlo(t)
            statistics(1)
            xn(4)
            item(0, 0, 0)
            xn(5)
            item(0, 0, 1)
            xlo(4)
            xn(6)
            xlo(5)
            item(0, 0, 2)
            xn(7)
            item(0, 0, 3)
            xlo(6)
            xlo(7)
            dve.wait_ge(lg_mm, 1)
            dve.wait_ge(small_in, 32)
            nc.vector.tensor_tensor(lg[:, :, :], p_y[:, 0:T * E].rearrange("p (t e) -> p t e", t=T),
                                    bg_b[:, :].unsqueeze(1).to_broadcast([P, T, E]), ALU.add).then_inc(lg_read, 1)
            dve.wait_ge(lg_read, 1)
            for t in range(T):
                ins = nc.vector.max(top[:, t, :], lg[:, t, :])
            link(ins)
            for t in range(T):
                ins = nc.vector.max_index(topi[:, t, :], top[:, t, :], lg[:, t, :])
            link(ins)
            link(nc.vector.tensor_copy(topf[:, :, :], topi[:, :, 0:2]))
            dve.wait_ge(consts, 1)
            for s in range(4):
                dve.wait_ge(xn_kept[s], 16 * (T // 4))
            dve.wait_ge(ln_t, T)
            n_tk = 2 * T

            def over(a, n, m):
                return a.unsqueeze(2).to_broadcast([P, n, m])

            def row(a, n, m):
                return a.unsqueeze(1).to_broadcast([P, n, m])

            link(nc.vector.tensor_tensor(is_top, row(iota_e[:, :], n_tk, E),
                                         over(topf[:, :, :].rearrange("p t k -> p (t k)"), n_tk, E), ALU.is_equal))
            by_k = is_top.rearrange("p (t k) e -> p t k e", k=2)
            nc.vector.tensor_tensor(member[:, :, :], by_k[:, :, 0, :], by_k[:, :, 1, :],
                                    ALU.add).then_inc(member_done, 1)
            item(0, 0, 4)
            dve.wait_ge(rank_mm, 1)
            ahead = p_out[:, 0:T * E].rearrange("p (t o e) -> p t o e", t=T, o=1).to_broadcast([P, T, 2, E])
            link(nc.vector.tensor_tensor(prod.rearrange("p (t k) e -> p t k e", k=2), by_k, ahead, ALU.mult))
            nc.vector.tensor_tensor(cmp_n, over(p_out[:, T * E:T * E + E], E, 8), row(steps[:, :], E, 8), ALU.is_gt)
            link(nc.vector.tensor_reduce(rank[:, :], prod, AX.X, ALU.add))
            nc.vector.tensor_reduce(tiles_e[:, :], cmp_n, AX.X, ALU.add)
            link(nc.vector.tensor_tensor(cmp_q, over(rank[:, :], n_tk, 7), row(steps[:, 1:8], n_tk, 7), ALU.is_ge))
            nc.vector.tensor_tensor(prod_e, before[:, :, :], row(tiles_e[:, :], E, E), ALU.mult)
            link(nc.vector.tensor_reduce(rfull[:, :], cmp_q, AX.X, ALU.add))
            nc.vector.scalar_tensor_tensor(pos[:, :], rfull[:, :], float(-P), rank[:, :], ALU.mult, ALU.add)
            link(nc.vector.tensor_reduce(tile0[:, :], prod_e, AX.X, ALU.add))
            item(0, 0, 5)
            nc.vector.tensor_tensor(prod2, is_top, row(tile0[:, :], n_tk, E), ALU.mult)
            link(nc.vector.tensor_tensor(tile1[:, :], tile0[:, :], tiles_e[:, :], ALU.add))
            nc.vector.tensor_tensor(cmp_t, over(iota_t[:, :], MT, E), row(tile1[:, :], MT, E), ALU.is_ge)
            link(nc.vector.tensor_reduce(rtile[:, :], prod2, AX.X, ALU.add))
            link(nc.vector.tensor_reduce(expert_f[:, :], cmp_t, AX.X, ALU.add))
            nc.vector.tensor_scalar(expert[:, :], expert_f[:, :], float(E - 1), None, ALU.min).then_inc(routed, 1)
            link(nc.vector.tensor_tensor(in_tile[:, :], rtile[:, :], rfull[:, :], ALU.add))
            nc.vector.tensor_tensor(is_tile, row(iota_t[:, :], n_tk, MT), over(in_tile[:, :], n_tk, MT), ALU.is_equal)
            nc.vector.tensor_scalar(off[:, :], pos[:, :], -1.0, lane[:, 0:1], ALU.mult, ALU.add).then_inc(tiles_done, 1)
            item(0, 0, 6)
            nc.vector.tensor_tensor(is_lane, row(iota_p, n_tk, P), over(pos[:, :], n_tk, P), ALU.is_equal).then_inc(lanes_done, 1)
            item(0, 1, 0)
            item(0, 1, 1)
            dve.wait_ge(table_mm, 1)
            part = p_out[:, P:P + 2 * MT]
            link(nc.vector.tensor_scalar(expert_f[:, :], part[:, 0:MT], lane_rows[:, 0:1], None, ALU.add))
            nc.vector.tensor_tensor(slot_token[:, :], part[:, MT:2 * MT], expert_f[:, :], ALU.add).then_inc(table_done, 1)

            def add_out(g, u, last):
                dve.wait_ge(out_mm, unit(g, u + 1))
                if last and u in SUM_FIRST:
                    dve.wait_ge(summed, SUM_FIRST.index(u) + 1)
                nc.vector.tensor_tensor(acc[:, u, :], p_out[:, :], acc[:, u, :], ALU.add).then_inc(out_acc, 1)

            def rows_lo(g, s, last):
                if tile_at(X_STEP, s, last) is not None:
                    dve.wait_ge(x_hi, tile(g, X_STEP[s]) + 1)
                    nc.vector.tensor_tensor(xgT[1][:, :, :].rearrange("p k c -> p (k c)"), p_y[:, :],
                                            F(xgT[0])[:, :, :].rearrange("p k c -> p (k c)"),
                                            ALU.subtract).then_inc(x_lo, 1)

            def light(s, last):
                return last and TB < s <= T

            def heads_lo(g, s):
                dve.wait_ge(o_hi, unit(g, s))
                nc.vector.tensor_tensor(oT[1][:, :, :].rearrange("p h (j q) -> p j h q", j=2),
                                        p_o[:, :].rearrange("p (j h q) -> p j h q", j=2, h=HG),
                                        F(oT[0])[:, :, :].rearrange("p h (j q) -> p j h q", j=2),
                                        ALU.subtract).then_inc(o_lo, 1)

            def a_pass(g, last):
                for s in range(STEPS):
                    mine = items_in(s, last)
                    ahead = int(s in ITEM_AHEAD)
                    for half, i in mine[:ahead]:
                        item(g, half, i)
                    if s < T:
                        dve.wait_ge(s_mm, unit(g, s + 1))
                        dve.wait_ge(pt_mm, unit(g, max(s - 1, 0)))
                        scores = pr[:, s % 2, :, :]
                        if s % TB == 0:
                            for jj in range(2):
                                at = slice(2 * jj, 2 * jj + 2)
                                ins = nc.vector.scalar_tensor_tensor(
                                    scores[:, at, :], p_small[:, at, :], SCALE,
                                    mask[:, jj:jj + 1, :].to_broadcast([P, 2, P]), ALU.mult, ALU.add)
                            ins.then_inc(s_masked, 1)
                        else:
                            nc.vector.scalar_tensor_tensor(scores, p_small, SCALE, mask[:, 1:2, :].to_broadcast([P, 4, P]),
                                                           ALU.mult, ALU.add).then_inc(s_masked, 1)
                        dve.wait_ge(s_masked, unit(g, s + 1))
                        nc.vector.scalar_tensor_tensor(scores, p_main, SCALE, scores, ALU.mult, ALU.add
                                                       ).then_inc(s_read, 1)
                        if light(s - 1, last):
                            heads_lo(g, s - 1)
                        dve.wait_ge(s_read, unit(g, s + 1))
                        nc.vector.tensor_reduce(nmax[:, s % 2, :], scores, AX.X, ALU.max, negate=True).then_inc(s_max, 1)
                    if s >= T and light(s - 1, last):
                        heads_lo(g, s - 1)
                    if 1 <= s <= T:
                        dve.wait_ge(pt_hi, unit(g, s))
                        nc.vector.tensor_tensor(pT[1][:, :, :, :].rearrange("p j h q -> p (j h q)"), p_pt[:, :],
                                                F(pT[0])[:, :, :, :].rearrange("p j h q -> p (j h q)"),
                                                ALU.subtract).then_inc(pt_lo, 1)
                    if s in X_EARLY:
                        rows_lo(g, s, last)
                    for half, i in mine[ahead:1]:
                        item(g, half, i)
                    sum_first = s > TB and not mine
                    if sum_first:
                        add_out(g, s - 2, last)
                    if s < T:
                        dve.wait_ge(p_exp, unit(g, s + 1))
                        nc.vector.reciprocal(rinv[:, :], rsum[:, s % 2, :]).then_inc(p_inv, 1)
                        dve.wait_ge(p_inv, unit(g, s + 1))
                        nc.vector.tensor_tensor(pr[:, s % 2, :, :], pr[:, s % 2, :, :], over(rinv[:, :], 4, P),
                                                ALU.mult).then_inc(p_norm, 1)
                    for half, i in mine[1:]:
                        item(g, half, i)
                    if s not in X_EARLY:
                        rows_lo(g, s, last)
                    if tile_at(Y_STEP, s, last) is not None:
                        c = Y_STEP[s]
                        dve.wait_ge(y_mm, tile(g, c) + 1)
                        dve.wait_ge(be_in, g * (16 * MP) + 16 * (c + 1))
                        nc.vector.tensor_tensor(p_y[:, :], p_y[:, :], be_b[:, :], ALU.add).then_inc(y_bias, 1)
                    if s >= 2 and not sum_first:
                        add_out(g, s - 2, last)
                    if 1 <= s <= T and not light(s, last):
                        heads_lo(g, s)

            with dve.Fori(0, G - 1) as g:
                a_pass(g, False)
            a_pass(G - 1, True)

        @block.tensor
        def _(pe):
            for signal in (s_mm, pt_mm, o_mm, out_mm, x_mm, y_mm):
                pe.sem_inc(signal, FREE)

            def product(out_ap, terms):
                n = 0
                for (ah, al), (bh, bl) in terms:
                    for a, b in ((ah, bh), (ah, bl), (al, bh)):
                        n += 1
                        ins = nc.tensor.matmul(out_ap, a, b, start=(n == 1), stop=(n == 3 * len(terms)))
                return ins

            def cut(halves, *index):
                return halves[0][index], halves[1][index]

            A = slice(None)

            def item(g, half, i, last=False):
                kind, n = ITEM[i]
                b = half % 2
                dst = p_item[(half * NI + i) % 2]
                if i == 0 and half in (0, 2):
                    pe.wait_ge(w_split, 1 if half == 0 else split_count(g, "kv"))
                if i == 3 and half in (0, 2):
                    pe.wait_ge(w_split, 2 if half == 0 else split_count(g, "q0"))
                if i == 5 and half in (0, 2):
                    pe.wait_ge(w_split, NF if half == 0 else split_count(g, "q1"))
                if half != 0 or i >= 2:
                    pe.wait_ge(item_out, nth(g, half, i if kind == "t" else i - 1))
                if kind == "t":
                    for c in range(TB):
                        ins = nc.tensor.transpose(dst[:, c * P:(c + 1) * P], vT[:, c * P:(c + 1) * P], ident[:, :])
                else:
                    w, m = {"k": (w_kv, 0), "v": (w_kv, 1), "q": (w_q, n)}[kind]
                    ins = product(dst[:, :], [(cut(w, A, m, k, A), cut(xT, A, k, slice(b * NTOK, (b + 1) * NTOK)))
                                              for k in range(KC)])
                ins.then_inc(item_mm, 1)

            def x_transposed(t):
                pe.wait_ge(ln_xn, t + 1)
                if t >= 4:
                    pe.wait_ge(ln_lo, t - 3)
                for k in range(KC):
                    ins = nc.tensor.transpose(p_ln[t % 4][:, k * P:(k + 1) * P], ring[:, t % 4, k * P:(k + 1) * P],
                                              ident[:, :])
                ins.then_inc(ln_t, 1)

            pe.wait_ge(ident_made, 1)
            for _ in range(WARM):
                nc.tensor.transpose(p_item[1][:, 0:P], ident[:, :], ident[:, :])
            for t in range(TB):
                x_transposed(t)
            for _ in range(WARM // 4):
                nc.tensor.transpose(p_item[1][:, 0:P], ident[:, :], ident[:, :])
            pe.wait_ge(ln_lo, TB)
            item(0, 0, 0)
            item(0, 0, 1)
            x_transposed(4)
            x_transposed(5)
            item(0, 0, 2)
            item(0, 0, 3)
            x_transposed(6)
            x_transposed(7)

            def logits(h):
                pe.wait_ge(ln_lo, (h + 1) * TB)
                for k in range(KC):
                    for n, a in enumerate(xT):
                        ins = nc.tensor.matmul(p_logit[h], xgT[0][:, k, :], a[:, k, h * 512:(h + 1) * 512],
                                               start=(k + n == 0), stop=(k + n == KC))
                ins.then_inc(lgT_mm, 1)

            pe.wait_ge(wg_done, 1)
            logits(0)
            logits(1)
            for t in range(T):
                pe.wait_ge(lgT_out, t // TB + 1)
                ins = nc.tensor.matmul(p_y[:, t * E:(t + 1) * E], lgT[:, t * P:(t + 1) * P], fold[:, :],
                                       start=True, stop=True)
            ins.then_inc(lg_mm, 1)
            item(0, 0, 4)
            pe.wait_ge(member_done, 1)
            for t in range(T - 1):
                n = T - 1 - t
                nc.tensor.matmul(p_out[:, (t + 1) * E:T * E], ones[:, :],
                                 member[:, t:t + 1, :].to_broadcast([P, n, E]), start=(t == 0), stop=False,
                                 skip_group_check=True)
            nc.tensor.matmul(p_out[:, 0:T * E], below[:, :], member[:, :, :].rearrange("p t e -> p (t e)"),
                             start=False, stop=True, skip_group_check=True)
            for t in range(T):
                ins = nc.tensor.matmul(p_out[:, T * E:T * E + E], ones[:, :], member[:, t, :],
                                       start=(t == 0), stop=(t == T - 1), skip_group_check=True)
            ins.then_inc(rank_mm, 1)
            for i in range(5, NI):
                item(0, 0, i)
            item(0, 1, 0)
            item(0, 1, 1)
            pe.wait_ge(lanes_done, 3)
            for a in range(2 * T):
                ins = nc.tensor.matmul(p_out[:, P:P + 2 * MT], is_lane[:, a, :],
                                       row_parts[:, a, :, :].rearrange("p h i -> p (h i)"),
                                       start=(a == 0), stop=(a == 2 * T - 1), skip_group_check=True)
            ins.then_inc(table_mm, 1)

            def expert(g, s, last):
                if tile_at(Y_STEP, s, last) is not None:
                    c = Y_STEP[s]
                    pe.wait_ge(w_split, split_count(g, f"e{c}b", last))
                    pe.wait_ge(x_lo, tile(g, c) + 1)
                    product(p_y[:, :], [(cut(xgT, A, k, A), cut(w_e, A, k, A)) for k in range(KC)]).then_inc(y_mm, 1)

            def a_pass(g, last):
                for s in range(STEPS):
                    mine = items_in(s, last)
                    ahead = int(s in ITEM_AHEAD)
                    for half, i in mine[:ahead]:
                        item(g, half, i)
                    if s < T:
                        b, t = divmod(s, TB)
                        pe.wait_ge(item_out, nth(g, 1 + b, 0))
                        pe.wait_ge(s_read, unit(g, s))
                        if s == 0:
                            pe.wait_ge(consts, 1)
                        for c in range(4):
                            j, hp = 2 * t + c // 2, c % 2
                            q_hi, q_lo = cut(qT, A, b, j, slice(2 * hp, 2 * hp + 2), A)
                            keys = slice(j * W, j * W + P)
                            nc.tensor.matmul(p_scores[:, c, :, :], q_hi, kT_both[:, :, b, keys],
                                             start=True, stop=False, skip_group_check=True)
                            ins = nc.tensor.matmul(p_small[:, c, :], q_lo, kT[0][:, b, keys],
                                                   start=False, stop=True, skip_group_check=True)
                        ins.then_inc(s_mm, 1)
                    if s in Y_AHEAD:
                        expert(g, s, last)
                    if 1 <= s <= T:
                        u = s - 1
                        pe.wait_ge(p_norm, unit(g, u + 1))
                        pe.wait_ge(pt_lo, unit(g, u))
                        for c in range(4):
                            ins = nc.tensor.transpose(p_pt[:, c * P:(c + 1) * P], pr[:, u % 2, c, :], ident[:, :])
                        ins.then_inc(pt_mm, 1)
                    late = len(mine) - int(s in ITEM_AHEAD)
                    for half, i in mine[ahead:late]:
                        item(g, half, i)
                    if tile_at(X_STEP, s, last) is not None:
                        c = X_STEP[s]
                        buf = XG_BUF[c]
                        per = XG_BUF.count(buf)
                        pe.wait_ge(xg_in[buf], g * (16 * per) + 16 * (XG_BUF[:c].count(buf) + 1))
                        pe.wait_ge(y_relu, tile(g, c))
                        for k in range(KC):
                            ins = nc.tensor.transpose(p_y[:, k * P:(k + 1) * P], xg[:, buf, k * P:(k + 1) * P],
                                                      ident[:, :])
                        ins.then_inc(x_mm, 1)
                    for half, i in mine[late:]:
                        item(g, half, i)
                    if s not in Y_AHEAD:
                        expert(g, s, last)
                    if s >= 2:
                        u = s - 2
                        if u == 0:
                            pe.wait_ge(w_split, split_count(g, "o1", last))
                        pe.wait_ge(out_acc, unit(g, u))
                        pe.wait_ge(o_hi, unit(g, u + 1))
                        for h in range(HG):
                            for n in range(2):
                                nc.tensor.matmul(p_out[:, :], oT[0][:, h, :], w_o[n][:, h, :],
                                                 start=(h + n == 0), stop=False)
                        pe.wait_ge(o_lo, unit(g, u + 1))
                        for h in range(HG):
                            ins = nc.tensor.matmul(p_out[:, :], oT[1][:, h, :], w_o[0][:, h, :],
                                                   start=False, stop=(h == HG - 1))
                        ins.then_inc(out_mm, 1)
                    if 1 <= s <= T:
                        u = s - 1
                        b, t = divmod(u, TB)
                        pe.wait_ge(pt_lo, unit(g, u + 1))
                        pe.wait_ge(o_lo, unit(g, u))
                        if t == 0:
                            pe.wait_ge(v_shifted, 48 * (2 * g + b + 1))
                        for jj in range(2):
                            ins = product(p_o[:, jj * 256:(jj + 1) * 256],
                                          [(cut(v, A, b, t, jj, A), cut(pT, A, jj, A, A))])
                        ins.then_inc(o_mm, 1)

            with pe.Fori(0, G - 1) as g:
                a_pass(g, False)
            a_pass(G - 1, True)


def kernel(**inputs):
    import numpy as np
    import concourse.bacc as bacc
    from concourse.bass_utils import run_bass_kernel_spmd as run

    def arr(name):
        return np.asarray(inputs[name])

    def heads(w, n):
        return np.ascontiguousarray(w.reshape(G, n, HD, KC, P).transpose(0, 4, 1, 3, 2).reshape(G, P, n * KC * HD))

    a = {
        "x": np.ascontiguousarray(arr("L0_attn_x").reshape(ROWS, DM)),
        "wq": heads(arr("L0_attn_wq"), HG),
        "wkv": np.concatenate([heads(arr("L0_attn_wk"), 1), heads(arr("L0_attn_wv"), 1)], axis=2),
        "wo": np.ascontiguousarray(arr("L0_attn_wo").reshape(DM, G, HG, HD).transpose(1, 3, 2, 0)
                                   .reshape(G, HD, HG * DM)),
        "wg": np.ascontiguousarray(arr("L0_ffn_W_gate")),
        "bg": np.ascontiguousarray(arr("L0_ffn_b_gate")),
        "we": np.ascontiguousarray(arr("L0_ffn_W_e").reshape(E, KC, P, DM).transpose(0, 2, 1, 3)
                                   .reshape(E, P, KC * DM)),
        "be": np.ascontiguousarray(arr("L0_ffn_b_e")),
    }
    nc = bacc.Bacc("TRN2", target_bir_lowering=False, num_devices=1)
    args = [nc.dram_tensor(f"in_{n}", v.shape, mybir.dt.from_np(v.dtype), kind="ExternalInput").ap()
            for n, v in a.items()]
    args.append(nc.dram_tensor("out_0", (ROWS, DM), mybir.dt.float32, kind="ExternalOutput").ap())
    build(nc, *args)
    r = run(nc, [{f"in_{n}": v for n, v in a.items()}], core_ids=[0])
    return r.results[0]["out_0"].reshape(NB, NTOK, DM)
```
